# Optimizing a Trainium2 kernel written in Bass

```python
import numpy as np
import jax
import jax.numpy as jnp

def _softmax(x, axis=-1):
    return jax.nn.softmax(x, axis=axis)

def _gelu(x):
    return jax.nn.gelu(x, approximate=True)

def _silu(x):
    return jax.nn.silu(x)

def _sigmoid(x):
    return jax.nn.sigmoid(x)

def _layernorm(x, axis=-1, eps=1e-05):
    m = jnp.mean(x, axis=axis, keepdims=True)
    v = jnp.var(x, axis=axis, keepdims=True)
    return (x - m) / jnp.sqrt(v + eps)

def _scatter_add(tgt, idx, src, axis=0):
    return tgt.at[idx].add(src)

def _segment_sum(src, seg, n):
    return jax.ops.segment_sum(src, seg, n)
kernel_name = 'mk_macaron_d1_jaxref_r4_2745a1'

def setup_inputs(seed: int=0):
    np.random.seed(seed)
    _w = jnp.asarray

    def _L0_attn_setup():
        import jax, jax.numpy as jnp
        import numpy as np
        import math
        B, S, E = (2, 512, 256)
        H, DC, DR = (16, 64, 128)
        HD = E // H

        def _linear_params(key, din, dout):
            k1, k2 = jax.random.split(key)
            bound = 1.0 / math.sqrt(din)
            w = jax.random.uniform(k1, (din, dout), minval=-bound, maxval=bound, dtype=jnp.float32)
            b = jax.random.uniform(k2, (dout,), minval=-bound, maxval=bound, dtype=jnp.float32)
            return (w, b)

        def _gelu(x):
            return jax.nn.gelu(x, approximate=False)

        def _rope_cos_sin(seq_len, d_rope):
            inv_freq = 1.0 / 10000.0 ** (jnp.arange(0, d_rope, 2, dtype=jnp.float32) / d_rope)
            t = jnp.arange(seq_len, dtype=jnp.float32)
            freqs = t[:, None] * inv_freq[None, :]
            emb = jnp.concatenate([freqs, freqs], axis=-1)
            return (jnp.cos(emb), jnp.sin(emb))

        def _apply_rope(x, cos, sin):
            d = x.shape[-1]
            x1, x2 = (x[..., :d // 2], x[..., d // 2:])
            rot = jnp.concatenate([-x2, x1], axis=-1)
            return x * cos + rot * sin
        key = jax.random.key(seed)
        ks = jax.random.split(key, 10)
        x = jax.random.normal(ks[0], (B, S, E), dtype=jnp.float32)
        wq, bq = _linear_params(ks[1], E, DC)
        wqc, bqc = _linear_params(ks[2], DC, E - DR)
        wqr, bqr = _linear_params(ks[3], E, DR)
        wkv, bkv = _linear_params(ks[4], E, DC)
        wkr, bkr = _linear_params(ks[5], E, DR)
        wkc, bkc = _linear_params(ks[6], DC, E - DR)
        wv, bv = _linear_params(ks[7], DC, E)
        wo, bo = _linear_params(ks[8], E, E)
        return dict(x=x, wq=wq, bq=bq, wqc=wqc, bqc=bqc, wqr=wqr, bqr=bqr, wkv=wkv, bkv=bkv, wkr=wkr, bkr=bkr, wkc=wkc, bkc=bkc, wv=wv, bv=bv, wo=wo, bo=bo)
    _L0_attn_in = _L0_attn_setup()

    def _L0_ffn_setup():
        import jax, jax.numpy as jnp
        import numpy as np
        B, T, C, E = (4, 512, 256, 8)
        key = jax.random.key(seed)
        k_x, k_wr, k_we = jax.random.split(key, 3)
        x = jax.random.normal(k_x, (B, T, C), dtype=jnp.float32)
        Wr = jax.random.normal(k_wr, (E, C), dtype=jnp.float32) * 0.05
        br = jnp.zeros((E,), dtype=jnp.float32)
        We = jax.random.normal(k_we, (E, C, C), dtype=jnp.float32) * (1.0 / np.sqrt(C))
        be = jnp.zeros((E, C), dtype=jnp.float32)
        return {'x': x, 'Wr': Wr, 'br': br, 'We': We, 'be': be}
    _L0_ffn_in = _L0_ffn_setup()
    _d = {'L0_attn_x': _L0_attn_in['x'], 'L0_attn_wq': _L0_attn_in['wq'], 'L0_attn_bq': _L0_attn_in['bq'], 'L0_attn_wqc': _L0_attn_in['wqc'], 'L0_attn_bqc': _L0_attn_in['bqc'], 'L0_attn_wqr': _L0_attn_in['wqr'], 'L0_attn_bqr': _L0_attn_in['bqr'], 'L0_attn_wkv': _L0_attn_in['wkv'], 'L0_attn_bkv': _L0_attn_in['bkv'], 'L0_attn_wkr': _L0_attn_in['wkr'], 'L0_attn_bkr': _L0_attn_in['bkr'], 'L0_attn_wkc': _L0_attn_in['wkc'], 'L0_attn_bkc': _L0_attn_in['bkc'], 'L0_attn_wv': _L0_attn_in['wv'], 'L0_attn_bv': _L0_attn_in['bv'], 'L0_attn_wo': _L0_attn_in['wo'], 'L0_attn_bo': _L0_attn_in['bo'], 'L0_ffn_Wr': _L0_ffn_in['Wr'], 'L0_ffn_br': _L0_ffn_in['br'], 'L0_ffn_We': _L0_ffn_in['We'], 'L0_ffn_be': _L0_ffn_in['be']}
    _x0 = _d['L0_attn_x']
    _d['L0_attn_x'] = jax.random.normal(jax.random.fold_in(jax.random.key(seed), 1), (2, 2048, 256), dtype=_x0.dtype)
    del _x0
    return _d

def reference(L0_attn_x, L0_attn_wq, L0_attn_bq, L0_attn_wqc, L0_attn_bqc, L0_attn_wqr, L0_attn_bqr, L0_attn_wkv, L0_attn_bkv, L0_attn_wkr, L0_attn_bkr, L0_attn_wkc, L0_attn_bkc, L0_attn_wv, L0_attn_bv, L0_attn_wo, L0_attn_bo, L0_ffn_Wr, L0_ffn_br, L0_ffn_We, L0_ffn_be):

    def _L0_attn_ref(x, wq, bq, wqc, bqc, wqr, bqr, wkv, bkv, wkr, bkr, wkc, bkc, wv, bv, wo, bo):
        import jax, jax.numpy as jnp
        import numpy as np
        import math
        B, S, E = (2, 512, 256)
        H, DC, DR = (16, 64, 128)
        HD = E // H

        def _linear_params(key, din, dout):
            k1, k2 = jax.random.split(key)
            bound = 1.0 / math.sqrt(din)
            w = jax.random.uniform(k1, (din, dout), minval=-bound, maxval=bound, dtype=jnp.float32)
            b = jax.random.uniform(k2, (dout,), minval=-bound, maxval=bound, dtype=jnp.float32)
            return (w, b)

        def _gelu(x):
            return jax.nn.gelu(x, approximate=False)

        def _rope_cos_sin(seq_len, d_rope):
            inv_freq = 1.0 / 10000.0 ** (jnp.arange(0, d_rope, 2, dtype=jnp.float32) / d_rope)
            t = jnp.arange(seq_len, dtype=jnp.float32)
            freqs = t[:, None] * inv_freq[None, :]
            emb = jnp.concatenate([freqs, freqs], axis=-1)
            return (jnp.cos(emb), jnp.sin(emb))

        def _apply_rope(x, cos, sin):
            d = x.shape[-1]
            x1, x2 = (x[..., :d // 2], x[..., d // 2:])
            rot = jnp.concatenate([-x2, x1], axis=-1)
            return x * cos + rot * sin
        b, s, _ = x.shape
        cq = _gelu(x @ wq + bq)
        q_c = cq @ wqc + bqc
        q_r = x @ wqr + bqr
        ckv = _gelu(x @ wkv + bkv)
        k_r = x @ wkr + bkr
        k_c = ckv @ wkc + bkc
        v = (ckv @ wv + bv).reshape(b, s, H, HD).transpose(0, 2, 1, 3)
        cos, sin = _rope_cos_sin(s, DR)
        q_r = _apply_rope(q_r, cos, sin)
        k_r = _apply_rope(k_r, cos, sin)
        q = _gelu(jnp.concatenate([q_c, q_r], axis=-1)).reshape(b, s, H, HD).transpose(0, 2, 1, 3)
        k = _gelu(jnp.concatenate([k_c, k_r], axis=-1)).reshape(b, s, H, HD).transpose(0, 2, 1, 3)
        scale = 1.0 / math.sqrt(HD)
        scores = jnp.einsum('bhqd,bhkd->bhqk', q, k) * scale
        causal = jnp.triu(jnp.ones((s, s), dtype=bool), k=1)
        scores = jnp.where(causal[None, None], -jnp.inf, scores)
        attn = jax.nn.softmax(scores, axis=-1)
        out = jnp.einsum('bhqk,bhkd->bhqd', attn, v)
        out = out.transpose(0, 2, 1, 3).reshape(b, s, E)
        return out @ wo + bo

    def _L0_ffn_ref(x, Wr, br, We, be):
        import jax, jax.numpy as jnp
        import numpy as np
        B, T, C, E = (4, 512, 256, 8)
        logits = jnp.einsum('btc,ec->bte', x, Wr) + br
        gates = jax.nn.softmax(logits, axis=-1)
        mask = (gates > 0.5).astype(x.dtype)
        h = jnp.einsum('btc,edc->bted', x, We) + be
        return jnp.einsum('bted,bte->btd', h, mask)
    x = L0_attn_x
    x = x + 0.5 * _L0_ffn_ref(_layernorm(x, axis=-1), L0_ffn_Wr, L0_ffn_br, L0_ffn_We, L0_ffn_be)
    x = x + _L0_attn_ref(_layernorm(x, axis=-1), L0_attn_wq, L0_attn_bq, L0_attn_wqc, L0_attn_bqc, L0_attn_wqr, L0_attn_bqr, L0_attn_wkv, L0_attn_bkv, L0_attn_wkr, L0_attn_bkr, L0_attn_wkc, L0_attn_bkc, L0_attn_wv, L0_attn_bv, L0_attn_wo, L0_attn_bo)
    x = x + 0.5 * _L0_ffn_ref(_layernorm(x, axis=-1), L0_ffn_Wr, L0_ffn_br, L0_ffn_We, L0_ffn_be)
    return x

_drawn_inputs = setup_inputs


def setup_inputs(seed=0):
    import zlib

    import numpy as np

    out = dict(_drawn_inputs(seed))
    spreads = {'L0_ffn_br': (0.0, 0.1), 'L0_ffn_be': (0.0, 0.309)}
    factors = {'L0_attn_wq': 8.0,
     'L0_attn_bq': 8.0,
     'L0_attn_wqc': 8.0,
     'L0_attn_bqc': 8.0,
     'L0_attn_wqr': 8.0,
     'L0_attn_bqr': 8.0,
     'L0_attn_wkv': 4.13,
     'L0_attn_bkv': 4.007,
     'L0_attn_wkr': 8.0,
     'L0_attn_bkr': 8.0,
     'L0_attn_wkc': 8.0,
     'L0_attn_bkc': 8.0}
    for name, (base, spread) in spreads.items():
        noise = np.random.default_rng([zlib.crc32(name.encode()), seed]).standard_normal(out[name].shape)
        drawn = base * np.exp(spread * noise) if base else spread * noise
        out[name] = jnp.asarray(drawn.astype(out[name].dtype))
    for name, factor in factors.items():
        out[name] = (out[name] * factor).astype(out[name].dtype)
    return out
```

```python
from contextlib import ExitStack

import concourse.bass as bass
from concourse import mybir

F32 = mybir.dt.float32
BF16 = mybir.dt.bfloat16
ALU = mybir.AluOpType
ACT = mybir.ActivationFunctionType
AX_X = mybir.AxisListType.X

P = 128
B, S, E = 2, 2048, 256
H, DC, HD = 16, 64, 16
NE = 8
KT = E // P
TOK = B * S
BLK = 512
NBLK = TOK // BLK
TPB = BLK // P
NT = TOK // P
NQB = S // BLK
NKT = S // P
HG = 4
NG = B * H // HG
GB = H // HG
PAIRS = HG // 2
VW = 32
FEAT = HG * HD
ROWS = 6 * HD
ROWS_M = ROWS + 3
EPS = 1e-5
SCALE = HD ** -0.5
MASKED = -3.0e38
CONSTS = 10
NPB = 4
RING = 4
Q_STACK = (0, 1, 2, 0, 1, 0)
K_STACK = (0, 0, 0, 1, 1, 2)
LOADS = len(Q_STACK) + len(K_STACK)
QUADS = [(i, j) for i in range(NQB) for j in range(TPB * i + TPB)]
NQ = len(QUADS)


def first_column(i, j):
    return P * max(0, j - TPB * i)


def plan_step(with_scores, with_max):
    base = []
    if with_scores:
        for n in range(NQ + 1):
            if n < NQ:
                width = BLK - first_column(*QUADS[n])
                base += [(("scores", n, p), 2 * width / 2.4) for p in range(PAIRS)]
            if n >= 1:
                i, j = QUADS[n - 1]
                base.append((("pv", n - 1), HG * (BLK - first_column(i, j)) * 0.46))
                if j == TPB * i + TPB - 1:
                    base.append((("o_out", i), 0.0))
                if j == 0 and i >= 1:
                    base.append((("o_turn", i - 1), 800.0))
        base.append((("o_turn", NQB - 1), 800.0))
    maxes = []
    if with_max:
        for h in range(HG):
            for i in range(NQB):
                for a in range(TPB):
                    for c in range(i + 1):
                        width = BLK if c < i else P * (a + 1)
                        maxes.append((("max", h, i, a, c, width), 62 + width / 0.96))
                maxes.append((("m_fold", h, i), 100.0))
        late, out = [], []
        for event in maxes:
            out.append(event)
            late = [(k - 1, e) for k, e in late]
            if late and late[0][0] == 0:
                out.append(late.pop(0)[1])
            if event[0][0] == "m_fold":
                late.append((2, (("m_turn", *event[0][1:]), 200.0)))
        maxes = out + [e for _, e in late]
    if not base:
        order = [e for e, _ in maxes]
    else:
        delay = 9000.0
        total, need = sum(c for _, c in base) - delay, sum(c for _, c in maxes)
        order, at, spent = [], 0.0, 0.0
        for event, cost in base:
            while maxes and spent < need * max(0.0, at - delay) / total:
                e, c = maxes.pop(0)
                order.append(e)
                spent += c
            order.append(event)
            at += cost
        order += [e for e, _ in maxes]
    slot, numbered = 0, []
    for event in order:
        if event[0] in ("max", "m_turn"):
            numbered.append((*event, slot))
            slot += 1
        elif event[0] == "m_fold":
            numbered.append((*event, slot))
        else:
            numbered.append(event)
    return numbered


STEPS = {"max": plan_step(False, True), "both": plan_step(True, True), "scores": plan_step(True, False)}
NMX = sum(e[0] in ("max", "m_turn") for e in STEPS["max"])


def run_steps(eng, one):
    one("max", 0, 0, 0)
    with eng.Fori(0, (NG - 2) // 2) as k:
        one("both", 1, 2 * k + 1, k)
        one("both", 0, 2 * k + 2, k + 1)
    one("both", 1, NG - 1, NG // 2 - 1)
    one("scores", 0, NG, NG // 2)


def build(nc, x, wcq, bcq, wqc, wkc, wr4, br4, bc2, wv, bv, wo, bo, wrt, br, wet, be, cos_t, sin_t, out):
    with ExitStack() as ctx:
        def sb(name, shape, dt):
            return ctx.enter_context(nc.sbuf_tensor(name, shape, dt))

        def sem(name):
            return ctx.enter_context(nc.semaphore(name))

        def dram(name, shape, dt):
            return nc.dram_tensor(name, shape, dt, kind="Internal").ap()

        psum = ctx.enter_context(nc.psum_tensor("psum", [P, 8, BLK], F32))

        x1_d = dram("x1_d", [TOK, E], F32)
        x2_d = dram("x2_d", [TOK, E], F32)
        q_d = dram("q_d", [3, B * E, S], BF16)
        k_d = dram("k_d", [3, B * E, S], BF16)
        v_d = dram("v_d", [NG, P, NKT, HG * VW], F32)
        att_d = dram("att_d", [NG, S, FEAT], F32)

        ident = sb("ident", [P, P], F32)
        ident_b = sb("ident_b", [P, P], BF16)
        mask_q = sb("mask_q", [P, P], BF16)
        mask_k = sb("mask_k", [P, P], BF16)
        ones_row = sb("ones_row", [1, P], F32)
        neg_half = sb("neg_half", [P, TPB], F32)
        over_e = sb("over_e", [P, TPB], F32)
        minus_over_e = sb("minus_over_e", [P, TPB], F32)
        eps_s = sb("eps_s", [P, TPB], F32)
        nought = sb("nought", [TPB, P], F32)

        wet_s = sb("wet_s", [P, KT, NE * E], F32)
        wrt_s = sb("wrt_s", [P, KT, NE], F32)
        br_s = sb("br_s", [1, NE], F32)
        be_s = sb("be_s", [NE, E], F32)
        wcq_s = sb("wcq_s", [P, KT, P], F32)
        wr4_s = sb("wr4_s", [P, KT, 4, P], F32)
        wc2_s = sb("wc2_s", [P, P], F32)
        wv_s = sb("wv_s", [P, E], F32)
        bcq_s = sb("bcq_s", [P, 1], F32)
        bc_s = sb("bc_s", [P, 2], F32)
        br4_s = sb("br4_s", [P, 4], F32)
        bv_s = sb("bv_s", [P, E], F32)
        wo_s = sb("wo_s", [P, KT, E], F32)
        bo_s = sb("bo_s", [P, E], F32)

        xt = sb("xt", [P, TPB, E], F32)
        xc = sb("xc", [P, TPB, E], F32)
        xn = sb("xn", [P, TPB, E], F32)
        unread = sb("unread", [P, TPB, E], F32)
        total = sb("total", [P, TPB], F32)
        neg_mean = sb("neg_mean", [P, TPB], F32)
        squares = sb("squares", [P, TPB], F32)
        mean_sq = sb("mean_sq", [P, TPB], F32)
        variance = sb("variance", [P, TPB], F32)
        rstd = sb("rstd", [P, TPB], F32)
        xnT = sb("xnT", [P, 2, KT, P], F32)
        neg_top = sb("neg_top", [P, 2], F32)
        esum = sb("esum", [P, 2], F32)
        rsum_e = sb("rsum_e", [P, 2], F32)
        expo = sb("expo", [P, 2, NE], F32)
        chosen = sb("chosen", [P, 2, NE], F32)
        half_mask = sb("half_mask", [P, 2, NE], F32)
        maskT = sb("maskT", [NE, 2, P], F32)
        yt = sb("yt", [P, TPB, E], F32)

        with ExitStack() as bctx:
            def sbb(name, shape, dt):
                return bctx.enter_context(nc.sbuf_tensor(name, shape, dt))
            cos_s = sbb("cos_s", [P, BLK], F32)
            sin_s = sbb("sin_s", [P, BLK], F32)
            xnT4 = sbb("xnT4", [P, KT, BLK], F32)
            ccT = sbb("ccT", [P, BLK], F32)
            by_cos = sbb("by_cos", [P, 2, BLK], F32)
            by_sin = sbb("by_sin", [P, 2, BLK], F32)
            turned = sbb("turned", [P, 2, BLK], F32)
            gel = sbb("gel", [P, 4, BLK], F32)
            rest = sbb("rest", [P, 4, BLK], F32)
            part = sbb("part", [P, 4, 3, BLK], BF16)
            vt = sbb("vt", [P, TPB, H, VW], F32)
            att = sbb("att", [P, TPB, GB, FEAT], F32)
            attT = sbb("attT", [P, 2, KT, P], F32)
            x1b = sbb("x1b", [P, 2, E], F32)

        qs = sb("qs", [P, 2, HG, S], BF16)
        ks = sb("ks", [P, 2, HG, S], BF16)
        vg = sb("vg", [P, 2, NKT, HG * VW], F32)
        prob = sb("prob", [P, NPB, HG, BLK], F32)
        pmax = sb("pmax", [P, RING, TPB, NQB], F32)
        nmax = sb("nmax", [P, RING, TPB], F32)
        mrow = sb("mrow", [TPB, RING, P], F32)
        mrest = sb("mrest", [TPB, RING, P], F32)
        mpart = sb("mpart", [TPB, RING, 3, P], BF16)
        osb = sb("osb", [P, BLK], F32)
        inv = sb("inv", [P, TPB, HG], F32)
        ob = sb("ob", [P, 2, TPB, FEAT], F32)

        s_const0 = sem("s_const0")
        s_const = sem("s_const")
        s_meet = [sem(f"s_meet{n}") for n in range(4)]
        s_ffw = sem("s_ffw")
        s_w = sem("s_w")

        def ffn_semaphores(tag):
            names = ("total", "negmean", "squares", "variance", "rstd", "xc", "xn", "xn_turned", "xnT",
                     "logit", "negtop", "exp", "rsum", "chosen", "mask", "mask_turned", "maskT", "experts",
                     "bias", "y")
            f = {k: sem(f"{tag}_{k}") for k in names}
            f["x_in"] = [sem(f"{tag}_x_in{t}") for t in range(TPB)]
            f["y_out"] = [sem(f"{tag}_y_out{t}") for t in range(TPB)]
            return f

        fa = ffn_semaphores("fa")
        fe = ffn_semaphores("fe")
        b_names = ("total", "negmean", "squares", "variance", "rstd", "xc", "xn", "xn_turned", "xnT", "cc_mm",
                   "cc", "rot_mm", "plain_mm", "v_mm", "by", "turned", "gel", "h", "rest", "m", "l", "v", "vpad")
        sbm = {k: sem(f"b_{k}") for k in b_names}
        b_x = [sem(f"b_x{t}") for t in range(TPB)]
        b_table = sem("b_table")
        b_out = sem("b_out")
        b_vout = sem("b_vout")

        c_stack = [[sem(f"c_stack{u}{h}") for h in range(HG)] for u in range(2)]
        c_v = [sem(f"c_v{u}") for u in range(2)]
        c_ones = sem("c_ones")
        c_scores = sem("c_scores")
        c_exp = sem("c_exp")
        c_pv = sem("c_pv")
        c_osb = sem("c_osb")
        c_oturn = sem("c_oturn")
        c_inv = sem("c_inv")
        c_ob = sem("c_ob")
        c_obst = [sem(f"c_obst{u}") for u in range(2)]
        c_mx = sem("c_mx")
        c_mxread = sem("c_mxread")
        c_fold = sem("c_fold")
        c_msplit = sem("c_msplit")
        c_mst = [[sem(f"c_mst{u}{i}") for i in range(NQB)] for u in range(2)]

        d_att = [sem(f"d_att{t}") for t in range(TPB)]
        d_x1 = [sem(f"d_x1{t}") for t in range(TPB)]
        d_turn = sem("d_turn")
        d_attT = sem("d_attT")
        d_proj = sem("d_proj")
        d_x1b = sem("d_x1b")
        d_x2 = sem("d_x2")
        d_out = [sem(f"d_out{t}") for t in range(TPB)]

        block = ctx.enter_context(nc.Block())

        def meet(eng, n):
            eng.drain().then_inc(s_meet[n], 1)
            eng.wait_ge(s_meet[n], 5)

        def uses(half, u):
            return half + u

        @block.sync
        def _(sp):
            def ffn_sync(f, src, dst):
                def blk(n, more):
                    for t in range(TPB):
                        v = TPB * n + t
                        sp.wait_ge(f["y"], 9 * v + 45)
                        sp.dma_start(dst[bass.ts(v, P), :], yt[:, t, :]).then_inc(f["y_out"][t], 16)
                        if more:
                            sp.dma_start(xt[:, t, :], src[bass.ts(v + TPB, P), :]).then_inc(f["x_in"][t], 16)

                for t in range(TPB):
                    sp.dma_start(xt[:, t, :], src[t * P:(t + 1) * P, :]).then_inc(f["x_in"][t], 16)
                with sp.Fori(0, NBLK - 1) as n:
                    blk(n, True)
                blk(NBLK - 1, False)
                for t in range(TPB):
                    sp.wait_ge(f["y_out"][t], 16 * NBLK + 16)

            for dst, src in ((wet_s[:, :, :], wet.rearrange("(k p) n -> p k n", p=P)),
                             (wrt_s[:, :, :], wrt.rearrange("(k p) n -> p k n", p=P)),
                             (br_s[:, :], br), (be_s[:, :], be)):
                sp.dma_start(dst, src).then_inc(s_ffw, 16)
            for dst, src in ((wcq_s[:, :, :], wcq.rearrange("(k p) n -> p k n", p=P)),
                             (wr4_s[:, :, :, :], wr4.rearrange("(k p) a n -> p k a n", p=P)),
                             (wc2_s[0:DC, :], wqc), (wc2_s[DC:P, :], wkc), (wv_s[DC:P, :], wv),
                             (bcq_s[:, :], bcq), (bc_s[:, :], bc2), (br4_s[:, :], br4),
                             (bv_s[:, :], bv.to_broadcast([P, E])),
                             (wo_s[:, :, :], wo.rearrange("(k p) n -> p k n", p=P)),
                             (bo_s[:, :], bo.to_broadcast([P, E]))):
                sp.dma_start(dst, src).then_inc(s_w, 16)
            ffn_sync(fa, x, x1_d)
            meet(sp, 0)

            def load_x1(row):
                for t in range(TPB):
                    sp.dma_start(xt[:, t, :], x1_d[bass.ds(row + t * P, P), :]).then_inc(b_x[t], 16)

            def b_sync(b, n, more):
                v = NQB * b + n
                row, nxt = sp.snap(n * BLK), sp.snap((v + 1) * BLK)
                sp.wait_ge(sbm["by"], 4 * v + 4)
                sp.dma_start(cos_s[:, :], cos_t[:, bass.ds(row, BLK)]).then_inc(b_table, 16)
                sp.dma_start(sin_s[:, :], sin_t[:, bass.ds(row, BLK)]).then_inc(b_table, 16)
                if more:
                    sp.wait_ge(sbm["xn"], TPB * v + 2 * TPB)
                    load_x1(nxt)
                sp.wait_ge(sbm["l"], 4 * v + 8)
                sp.wait_ge(sbm["v"], TPB * v + 2 * TPB)
                for g in range(GB):
                    sp.dma_start(v_d[bass.ds(b * GB + g, 1), :, bass.ts(n, TPB), :].rearrange("o p t f -> p (o t) f"),
                                 vt[:, :, g * HG:(g + 1) * HG, :].rearrange("p t h w -> p t (h w)")
                                 ).then_inc(b_vout, 16)
                for a in range(4):
                    dst = (q_d, k_d)[a % 2]
                    for r in range(3):
                        sp.dma_start(dst[r, bass.ds(b * E + (a // 2) * P, P), bass.ds(row, BLK)],
                                     part[:, a, r, :]).then_inc(b_out, 16)

            load_x1(0)
            for b in range(B):
                with sp.Fori(0, NQB - 1) as n:
                    b_sync(b, n, True)
                b_sync(b, NQB - 1, b < B - 1)
            sp.wait_ge(b_out, 16 * 12 * (NBLK + 1))
            sp.wait_ge(b_vout, 16 * GB * (NBLK + 1))
            meet(sp, 1)

            def load_group(u, g):
                for h in range(HG):
                    for dst, src, stack in ((qs, q_d, Q_STACK), (ks, k_d, K_STACK)):
                        for row, r in enumerate(stack):
                            sp.dma_start(dst[row * HD:(row + 1) * HD, u, h, :],
                                         src[r, bass.ds(g * FEAT + h * HD, HD), :]).then_inc(c_stack[u][h], 16)
                sp.dma_start(vg[:, u, :, :], v_d[bass.ds(g, 1), :, :, :].rearrange("o p j f -> p (o j) f")
                             ).then_inc(c_v[u], 16)

            def sync_step(kind, u, s, half):
                for e in STEPS[kind]:
                    if e[0] == "m_turn":
                        _, h, i, _ = e
                        k = HG * NQB * s + NQB * h + i
                        sp.wait_ge(c_msplit, 4 * k + 4)
                        for r in range(3):
                            sp.dma_start(qs[ROWS + r:ROWS + r + 1, u, h, i * BLK:(i + 1) * BLK],
                                         mpart[:, i % RING, r, :]).then_inc(c_mst[u][i], 16)
                    elif e[0] == "o_turn":
                        i = e[1]
                        sp.wait_ge(c_ob, NQB * (s - 1) + i + 2)
                        sp.dma_start(att_d[bass.ds(s - 1, 1), i * BLK:(i + 1) * BLK, :].rearrange(
                                         "o (a p) f -> p (o a) f", p=P),
                                     ob[:, i % 2, :, :]).then_inc(c_obst[i % 2], 16)
                if kind == "max":
                    load_group(1, 1)
                elif kind == "both" and not (isinstance(s, int) and s == NG - 1):
                    sp.wait_ge(c_pv, NQ * s + NPB)
                    load_group(1 - u, s + 1)

            load_group(0, 0)
            run_steps(sp, sync_step)
            for u in range(2):
                sp.wait_ge(c_obst[u], 16 * NG * NQB // 2 + 16)
            meet(sp, 2)

            with sp.Fori(0, B) as b:
                with sp.Fori(0, NQB) as n:
                    for t in range(TPB):
                        v = (NQB * b + n) * TPB + t
                        sp.wait_ge(d_x2, v + 1)
                        sp.dma_start(att[:, t, :, :], att_d[bass.ds(b * GB, GB), bass.ds(n * BLK + t * P, P), :]
                                     .rearrange("g p f -> p g f")).then_inc(d_att[t], 16)
                        sp.dma_start(xt[:, t, :], x1_d[bass.ts(v, P), :]).then_inc(d_x1[t], 16)
                    for t in range(TPB):
                        v = (NQB * b + n) * TPB + t
                        sp.wait_ge(d_x2, v + 1 + TPB)
                        sp.dma_start(x2_d[bass.ts(v, P), :], yt[:, t, :]).then_inc(d_out[t], 16)
            for t in range(TPB):
                sp.wait_ge(d_out[t], 16 * NBLK + 16)
            meet(sp, 3)
            ffn_sync(fe, x2_d, out)

        @block.gpsimd
        def _(pool):
            pool.memset(ident[:, :], 0.0).then_inc(s_const0, 1)
            pool.memset(mask_q[:, :], 0.0).then_inc(s_const0, 1)
            pool.memset(mask_k[:, :], 0.0).then_inc(s_const0, 1)
            pool.memset(ones_row[:, :], 1.0).then_inc(s_const, 1)
            pool.memset(neg_half[:, :], -0.5).then_inc(s_const, 1)
            pool.memset(over_e[:, :], 1.0 / E).then_inc(s_const, 1)
            pool.memset(minus_over_e[:, :], -1.0 / E).then_inc(s_const, 1)
            pool.memset(eps_s[:, :], EPS).then_inc(s_const, 1)
            pool.memset(nought[:, :], 0.0).then_inc(s_const, 1)
            pool.wait_ge(s_const0, 3)
            pool.affine_select(out=ident[:, :], in_=ident[:, :], compare_op=ALU.not_equal, fill=1.0, base=0,
                               pattern=[[-1, P]], channel_multiplier=1).then_inc(s_const, 1)
            pool.affine_select(out=mask_q[:, :], in_=mask_q[:, :], compare_op=ALU.is_ge, fill=MASKED, base=0,
                               pattern=[[-1, P]], channel_multiplier=1).then_inc(s_const, 1)
            pool.affine_select(out=mask_k[:, :], in_=mask_k[:, :], compare_op=ALU.is_ge, fill=MASKED, base=0,
                               pattern=[[1, P]], channel_multiplier=-1).then_inc(s_const, 1)
            pool.wait_ge(s_const, CONSTS - 1)
            pool.tensor_copy(ident_b[:, :], ident[:, :]).then_inc(s_const, 1)

            def statistics(f, t0, t1, v):
                n = t1 - t0
                pool.wait_ge(f["total"], n * v + n)
                pool.tensor_tensor(neg_mean[:, t0:t1], total[:, t0:t1], minus_over_e[:, 0:n],
                                   ALU.mult).then_inc(f["negmean"], 1)
                pool.wait_ge(f["squares"], n * v + n)
                pool.tensor_tensor(mean_sq[:, t0:t1], squares[:, t0:t1], over_e[:, 0:n],
                                   ALU.mult).then_inc(f["variance"], 1)
                pool.wait_ge(f["variance"], 2 * v + 1)
                pool.tensor_tensor(variance[:, t0:t1], mean_sq[:, t0:t1], eps_s[:, 0:n],
                                   ALU.add).then_inc(f["variance"], 1)
                pool.wait_ge(f["variance"], 2 * v + 2)
                pool.tensor_tensor(rstd[:, t0:t1], variance[:, t0:t1], neg_half[:, 0:n],
                                   ALU.pow).then_inc(f["rstd"], 1)

            def ffn_pool(f):
                with pool.Fori(0, NBLK) as n:
                    for t in range(TPB):
                        statistics(f, t, t + 1, TPB * n + t)

            ffn_pool(fa)
            meet(pool, 0)

            pool.sem_inc(sbm["turned"], 2)
            pool.memset(vt[:, :, :, HD:VW], 0.0).then_inc(sbm["vpad"], 1)
            pool.wait_ge(sbm["vpad"], 1)
            pool.memset(vt[:, :, :, HD:HD + 1], 1.0).then_inc(sbm["vpad"], 1)
            statistics(sbm, 0, TPB, 0)

            def b_pool(v, more):
                if more:
                    statistics(sbm, 0, TPB, v + 1)
                for z in range(2):
                    pool.wait_ge(sbm["by"], 4 * v + 2 * z + 6)
                    pool.wait_ge(sbm["gel"], 4 * v + 4)
                    pool.tensor_tensor(turned[:, z, :], by_cos[:, z, :], by_sin[:, z, :],
                                       ALU.add).then_inc(sbm["turned"], 1)
                for a in range(4):
                    pool.wait_ge(sbm["h"], 4 * v + a + 1)
                    pool.tensor_tensor(rest[:, a, :], gel[:, a, :], part[:, a, 0, :],
                                       ALU.subtract).then_inc(sbm["rest"], 1)

            with pool.Fori(0, NBLK - 1) as v:
                b_pool(v, True)
            b_pool(NBLK - 1, False)
            meet(pool, 1)

            for u in range(2):
                for h in range(HG):
                    pool.memset(ks[ROWS:ROWS_M, u, h, :], 1.0).then_inc(c_ones, 1)

            def pool_step(kind, u, s, half):
                for e in STEPS[kind]:
                    if e[0] != "m_turn":
                        continue
                    _, h, i, slot = e
                    k = HG * NQB * s + NQB * h + i
                    r = i % RING
                    pool.wait_ge(c_mxread, NMX * s + slot + 1)
                    if h > 0:
                        pool.wait_ge(c_mst[u][i], 48 * (HG * half + h))
                    elif not (isinstance(s, int) and s == 0):
                        pool.wait_ge(c_mst[1 - u][i], 48 * HG * uses(half, u))
                    pool.tensor_tensor(mpart[:, r, 0, :], mrow[:, r, :], nought[:, :],
                                       ALU.subtract).then_inc(c_msplit, 1)
                    pool.wait_ge(c_msplit, 4 * k + 1)
                    pool.tensor_tensor(mrest[:, r, :], mrow[:, r, :], mpart[:, r, 0, :],
                                       ALU.subtract).then_inc(c_msplit, 1)
                    pool.wait_ge(c_msplit, 4 * k + 2)
                    pool.tensor_tensor(mpart[:, r, 1, :], mrest[:, r, :], nought[:, :],
                                       ALU.subtract).then_inc(c_msplit, 1)
                    pool.wait_ge(c_msplit, 4 * k + 3)
                    pool.tensor_tensor(mpart[:, r, 2, :], mrest[:, r, :], mpart[:, r, 1, :],
                                       ALU.subtract).then_inc(c_msplit, 1)

            run_steps(pool, pool_step)
            meet(pool, 2)

            with pool.Fori(0, NBLK) as n:
                for t in range(TPB):
                    v = TPB * n + t
                    pool.wait_ge(d_x1[t], 16 * n + 16)
                    pool.wait_ge(d_x2, v + TPB - 1)
                    pool.tensor_tensor(x1b[:, t % 2, :], xt[:, t, :], bo_s[:, :], ALU.add).then_inc(d_x1b, 1)
            meet(pool, 3)
            ffn_pool(fe)

        @block.scalar
        def _(act):
            def normalise(f, x_in, t0, t1, v, n):
                k = t1 - t0
                for t in range(t0, t1):
                    act.wait_ge(x_in[t], 16 * n + 16)
                    act.activation(unread[:, t, :], xt[:, t, :], ACT.Identity,
                                   accum_out=total[:, t:t + 1]).then_inc(f["total"], 1)
                act.wait_ge(f["negmean"], v + 1)
                for t in range(t0, t1):
                    act.activation(xc[:, t, :], xt[:, t, :], ACT.Identity,
                                   bias=neg_mean[:, t:t + 1]).then_inc(f["xc"], 1)
                for t in range(t0, t1):
                    act.wait_ge(f["xc"], k * v + t - t0 + 1)
                    act.activation(unread[:, t, :], xc[:, t, :], ACT.Square,
                                   accum_out=squares[:, t:t + 1]).then_inc(f["squares"], 1)
                act.wait_ge(f["rstd"], v + 1)
                for t in range(t0, t1):
                    act.mul(xn[:, t, :], xc[:, t, :], rstd[:, t:t + 1]).then_inc(f["xn"], 1)

            def ffn_scalar(f):
                act.wait_ge(s_const, CONSTS)
                act.sem_inc(f["xnT"], 2)

                def blk(n, last):
                    for t in range(TPB):
                        v, u = TPB * n + t, t % 2
                        act.wait_ge(f["xn_turned"], v + 1)
                        act.wait_ge(f["experts"], v + 1)
                        act.copy(xnT[:, u, :, :], psum[:, 4 + u, 0:E].rearrange("p (k m) -> p k m", k=KT)
                                 ).then_inc(f["xnT"], 1)
                        act.wait_ge(f["negtop"], v + 1)
                        act.activation(expo[:, u, :], psum[:, 6 + u, E:E + NE], ACT.Exp, bias=neg_top[:, u:u + 1],
                                       accum_out=esum[:, u:u + 1]).then_inc(f["exp"], 1)
                        if t + 1 < TPB:
                            normalise(f, f["x_in"], t + 1, t + 2, v + 1, n)
                        elif not last:
                            normalise(f, f["x_in"], 0, 1, v + 1, n + 1)
                        act.wait_ge(f["mask_turned"], v + 1)
                        act.copy(maskT[:, u, :], psum[0:NE, 6 + u, 384:512]).then_inc(f["maskT"], 1)

                normalise(f, f["x_in"], 0, 1, 0, 0)
                with act.Fori(0, NBLK - 1) as n:
                    blk(n, False)
                blk(NBLK - 1, True)

            ffn_scalar(fa)
            meet(act, 0)

            act.wait_ge(s_w, 16 * 11)
            act.sem_inc(sbm["xn"], TPB)
            act.sem_inc(sbm["xnT"], 1)

            def b_scalar(v, more):
                act.wait_ge(sbm["xn_turned"], v + 1)
                act.wait_ge(sbm["rot_mm"], 4 * v + 4)
                act.copy(xnT4[:, :, :], psum[:, 0:KT, :]).then_inc(sbm["xnT"], 1)
                act.wait_ge(sbm["cc_mm"], v + 1)
                act.wait_ge(sbm["v_mm"], TPB * v + TPB)
                act.activation(ccT[:, :], psum[:, 2, :], ACT.Gelu, bias=bcq_s[:, :]).then_inc(sbm["cc"], 1)
                if more:
                    normalise(sbm, b_x, 0, TPB, v + 1, v + 1)
                act.wait_ge(b_out, 16 * 12 * (v + 1))
                act.wait_ge(sbm["l"], 4 * v + 4)
                for z in range(2):
                    act.wait_ge(sbm["plain_mm"], 2 * v + z + 1)
                    act.activation(gel[:, z, :], psum[:, z, :], ACT.Gelu, bias=bc_s[:, z:z + 1]
                                   ).then_inc(sbm["gel"], 1)
                for z in range(2):
                    act.wait_ge(sbm["turned"], 2 * v + z + 3)
                    act.activation(gel[:, 2 + z, :], turned[:, z, :], ACT.Gelu).then_inc(sbm["gel"], 1)
                for a in range(4):
                    act.wait_ge(sbm["gel"], 4 * v + a + 5)
                    act.copy(part[:, a, 0, :], gel[:, a, :]).then_inc(sbm["h"], 1)
                for a in range(4):
                    act.wait_ge(sbm["rest"], 4 * v + a + 1)
                    act.copy(part[:, a, 1, :], rest[:, a, :]).then_inc(sbm["m"], 1)

            normalise(sbm, b_x, 0, TPB, 0, 0)
            with act.Fori(0, NBLK - 1) as v:
                b_scalar(v, True)
            b_scalar(NBLK - 1, False)
            meet(act, 1)

            act.sem_inc(c_exp, 2)
            act.sem_inc(c_osb, 1)

            def scalar_step(kind, u, s, half):
                for e in STEPS[kind]:
                    if e[0] == "scores":
                        _, n, p = e
                        v = NQ * (s - 1) + n
                        c0 = first_column(*QUADS[n])
                        act.wait_ge(c_scores, 2 * v + p + 1)
                        act.wait_ge(c_pv, v + 1)
                        act.activation(prob[:, n % NPB, 2 * p:2 * p + 2, c0:BLK], psum[:, 2 * p:2 * p + 2, c0:BLK],
                                       ACT.Exp, scale=SCALE).then_inc(c_exp, 1)
                    elif e[0] == "o_out":
                        i = e[1]
                        w = NQB * (s - 1) + i
                        act.wait_ge(c_pv, NQ * (s - 1) + QUADS.index((i, TPB * i + TPB - 1)) + 1 + NPB)
                        act.wait_ge(c_oturn, w + 1)
                        act.copy(osb[:, :], psum[:, 6, :]).then_inc(c_osb, 1)

            run_steps(act, scalar_step)
            meet(act, 2)

            act.sem_inc(d_attT, 2)
            with act.Fori(0, NBLK) as n:
                for t in range(TPB):
                    v, u = TPB * n + t, t % 2
                    act.wait_ge(d_turn, v + 1)
                    act.wait_ge(d_proj, v + 1)
                    act.copy(attT[:, u, :, :], psum[:, 4 + u, 0:E].rearrange("p (k m) -> p k m", k=KT)
                             ).then_inc(d_attT, 1)
            meet(act, 3)
            ffn_scalar(fe)

        @block.tensor
        def _(pe):
            def ffn_tensor(f):
                pe.wait_ge(s_const, CONSTS)
                pe.wait_ge(s_ffw, 64)
                pe.sem_inc(f["experts"], 2)
                with pe.Fori(0, NBLK) as n:
                    for t in range(TPB):
                        v, u = TPB * n + t, t % 2
                        pe.wait_ge(f["xn"], v + 1)
                        pe.wait_ge(f["xnT"], v + 1)
                        for k in range(KT):
                            last = pe.transpose(psum[:, 4 + u, k * P:(k + 1) * P], xn[:, t, k * P:(k + 1) * P],
                                                ident[:, :])
                        last.then_inc(f["xn_turned"], 1)
                        pe.wait_ge(f["xnT"], v + 3)
                        for c in range(NE // 2):
                            pe.wait_ge(f["y"], 9 * v + 2 * c + 29)
                            for k in range(KT):
                                last = pe.matmul(psum[:, c, :], xnT[:, u, k, :],
                                                 wet_s[:, k, c * BLK:(c + 1) * BLK],
                                                 start=(k == 0), stop=(k == KT - 1))
                            if c == NE // 2 - 1:
                                last.then_inc(f["experts"], 1)
                            else:
                                last.then_inc(f["bias"], 1)
                            if c == 0:
                                pe.wait_ge(f["y"], 9 * v + 27)
                                for k in range(KT):
                                    pe.matmul(psum[:, 6 + u, E:E + NE], xnT[:, u, k, :], wrt_s[:, k, :],
                                              start=(k == 0), stop=False)
                                pe.matmul(psum[:, 6 + u, E:E + NE], ones_row[:, :], br_s[:, :],
                                          start=False, stop=True).then_inc(f["logit"], 1)
                        pe.wait_ge(f["mask"], v + 1)
                        pe.wait_ge(f["exp"], v + 1)
                        pe.transpose(psum[0:NE, 6 + u, 384:512], half_mask[:, u, :], ident[:, :]
                                     ).then_inc(f["mask_turned"], 1)
                        pe.wait_ge(f["maskT"], v + 1)
                        pe.matmul(psum[:, 6 + u, 0:E], maskT[:, u, :], be_s[:, :], start=True, stop=True
                                  ).then_inc(f["bias"], 1)

            ffn_tensor(fa)
            meet(pe, 0)

            pe.wait_ge(s_w, 16 * 11)
            pe.sem_inc(sbm["rot_mm"], 4)
            pe.sem_inc(sbm["v_mm"], TPB)
            with pe.Fori(0, NBLK) as v:
                pe.wait_ge(sbm["xn"], TPB * v + 2 * TPB)
                pe.wait_ge(sbm["gel"], 4 * v + 4)
                for k in range(KT):
                    for t in range(TPB):
                        last = pe.transpose(psum[:, k, t * P:(t + 1) * P], xn[:, t, k * P:(k + 1) * P], ident[:, :])
                last.then_inc(sbm["xn_turned"], 1)
                pe.wait_ge(sbm["xnT"], v + 2)
                pe.wait_ge(sbm["v"], TPB * v + TPB)
                for k in range(KT):
                    last = pe.matmul(psum[:, 2, :], wcq_s[:, k, :], xnT4[:, k, :], start=(k == 0), stop=(k == KT - 1))
                last.then_inc(sbm["cc_mm"], 1)
                pe.wait_ge(sbm["by"], 4 * v + 4)
                for a in range(4):
                    for k in range(KT):
                        last = pe.matmul(psum[:, 3 + a, :], wr4_s[:, k, a, :], xnT4[:, k, :],
                                         start=(k == 0), stop=(k == KT - 1))
                    last.then_inc(sbm["rot_mm"], 1)
                pe.wait_ge(sbm["cc"], v + 1)
                for z in range(2):
                    pe.matmul(psum[:, z, :], wc2_s[z * DC:(z + 1) * DC, :], ccT[z * DC:(z + 1) * DC, :],
                              start=True, stop=True).then_inc(sbm["plain_mm"], 1)
                for t in range(TPB):
                    bank, c0 = (7, 2)[t // 2], (t % 2) * E
                    pe.matmul(psum[:, bank, c0:c0 + E], ccT[DC:P, t * P:(t + 1) * P], wv_s[DC:P, :],
                              start=True, stop=True).then_inc(sbm["v_mm"], 1)
            meet(pe, 1)

            pe.wait_ge(c_ones, 2 * HG)
            pe.sem_inc(c_pv, NPB)
            pe.sem_inc(c_oturn, 1)

            def tensor_step(kind, u, s, half):
                w = 1 - u
                for e in STEPS[kind]:
                    if e[0] == "max":
                        _, h, i, a, c, width, slot = e
                        v = NMX * s + slot
                        if i == 0 and a == 0:
                            pe.wait_ge(c_stack[u][h], 16 * LOADS * (half + 1))
                        if not (isinstance(v, int) and v < 2):
                            pe.wait_ge(c_mxread, v - 1)
                        q0 = (TPB * i + a) * P
                        last = pe.matmul(psum[:, 4 + slot % 2, 0:width], qs[0:ROWS, u, h, q0:q0 + P],
                                         ks[0:ROWS, u, h, c * BLK:c * BLK + width], start=True, stop=(c < i))
                        if c == i:
                            last = pe.matmul(psum[:, 4 + slot % 2, width - P:width], ident_b[:, :], mask_q[:, :],
                                             start=False, stop=True)
                        last.then_inc(c_mx, 1)
                    elif e[0] == "m_turn":
                        _, h, i, slot = e
                        v = NMX * s + slot
                        pe.wait_ge(c_fold, HG * NQB * s + NQB * h + i + 1)
                        pe.wait_ge(c_mxread, v - 1)
                        pe.transpose(psum[0:TPB, 4 + slot % 2, 0:P], nmax[:, i % RING, :], ident[:, :]
                                     ).then_inc(c_mx, 1)
                    elif e[0] == "scores":
                        _, n, p = e
                        i, j = QUADS[n]
                        c0 = first_column(i, j)
                        if j == 0 and p == 0:
                            pe.wait_ge(c_mst[w][i], 48 * HG * uses(half, u))
                        pe.wait_ge(c_exp, 2 * (NQ * (s - 1) + n) + p + 1)
                        for h in (2 * p, 2 * p + 1):
                            last = pe.matmul(psum[:, h, c0:BLK], ks[0:ROWS_M, w, h, j * P:(j + 1) * P],
                                             qs[0:ROWS_M, w, h, i * BLK + c0:(i + 1) * BLK],
                                             start=True, stop=(j < TPB * i))
                            if j >= TPB * i:
                                last = pe.matmul(psum[:, h, c0:c0 + P], ident_b[:, :], mask_k[:, :],
                                                 start=False, stop=True)
                        last.then_inc(c_scores, 1)
                    elif e[0] == "pv":
                        n = e[1]
                        i, j = QUADS[n]
                        c0 = first_column(i, j)
                        if n == 0:
                            pe.wait_ge(c_v[w], 16 * uses(half, u))
                        if j == 0:
                            pe.wait_ge(c_osb, NQB * (s - 1) + i + 1)
                        pe.wait_ge(c_exp, 2 * (NQ * (s - 1) + n) + 4)
                        for h in range(HG):
                            last = pe.matmul(psum[h * VW:(h + 1) * VW, 6, c0:BLK],
                                             vg[:, w, j, h * VW:(h + 1) * VW], prob[:, n % NPB, h, c0:BLK],
                                             start=(j == 0), stop=(j == TPB * i + TPB - 1), skip_group_check=True)
                        last.then_inc(c_pv, 1)
                    elif e[0] == "o_turn":
                        i = e[1]
                        v = NQB * (s - 1) + i
                        pe.wait_ge(c_osb, v + 2)
                        pe.wait_ge(c_ob, v + 1)
                        for a in range(TPB):
                            last = pe.transpose(psum[:, 7, a * P:(a + 1) * P], osb[:, a * P:(a + 1) * P], ident[:, :])
                        last.then_inc(c_oturn, 1)

            run_steps(pe, tensor_step)
            meet(pe, 2)

            pe.sem_inc(d_proj, 2)
            with pe.Fori(0, NBLK) as n:
                for t in range(TPB):
                    v, u = TPB * n + t, t % 2
                    pe.wait_ge(d_att[t], 16 * n + 16)
                    pe.wait_ge(d_attT, v + 1)
                    for k in range(KT):
                        last = pe.transpose(psum[:, 4 + u, k * P:(k + 1) * P],
                                            att[:, t, 2 * k:2 * k + 2, :].rearrange("p g f -> p (g f)"), ident[:, :])
                    last.then_inc(d_turn, 1)
                    pe.wait_ge(d_attT, v + 3)
                    pe.wait_ge(d_x2, v + TPB - 1)
                    for k in range(KT):
                        last = pe.matmul(psum[:, 6 + u, 0:E], attT[:, u, k, :], wo_s[:, k, :],
                                         start=(k == 0), stop=(k == KT - 1))
                    last.then_inc(d_proj, 1)
            meet(pe, 3)
            ffn_tensor(fe)

        @block.vector
        def _(dve):
            def ffn_vector(f):
                dve.sem_inc(f["y"], 36)
                for t in range(TPB):
                    dve.sem_inc(f["y_out"][t], 16)
                with dve.Fori(0, NBLK) as n:
                    for t in range(TPB):
                        v, u = TPB * n + t, t % 2
                        dve.wait_ge(f["logit"], v + 1)
                        dve.reduce_max(neg_top[:, u:u + 1], psum[:, 6 + u, E:E + NE], AX_X,
                                       negate=True).then_inc(f["negtop"], 1)
                        dve.wait_ge(f["exp"], v + 1)
                        dve.reciprocal(rsum_e[:, u:u + 1], esum[:, u:u + 1]).then_inc(f["rsum"], 1)
                        dve.wait_ge(f["rsum"], v + 1)
                        dve.tensor_scalar(chosen[:, u, :], expo[:, u, :], rsum_e[:, u:u + 1], 0.5, ALU.mult,
                                          ALU.is_gt).then_inc(f["chosen"], 1)
                        dve.wait_ge(f["chosen"], v + 1)
                        dve.tensor_scalar(half_mask[:, u, :], chosen[:, u, :], 0.5, None,
                                          ALU.mult).then_inc(f["mask"], 1)
                        dve.wait_ge(f["mask"], v + 1)
                        dve.wait_ge(f["y_out"][t], 16 * n + 16)
                        for e in range(NE):
                            c = e // 2
                            if e == NE - 2:
                                dve.wait_ge(f["experts"], v + 3)
                            elif e % 2 == 0:
                                dve.wait_ge(f["bias"], 4 * v + c + 1)
                            if e:
                                dve.wait_ge(f["y"], 9 * v + e + 36)
                            dve.scalar_tensor_tensor(
                                out=yt[:, t, :], in0=psum[:, c, (e % 2) * E:(e % 2 + 1) * E],
                                scalar=half_mask[:, u, e:e + 1], in1=(yt if e else xt)[:, t, :],
                                op0=ALU.mult, op1=ALU.add).then_inc(f["y"], 1)
                        dve.wait_ge(f["bias"], 4 * v + 4)
                        dve.wait_ge(f["y"], 9 * v + 8 + 36)
                        dve.tensor_tensor(yt[:, t, :], psum[:, 6 + u, 0:E], yt[:, t, :], ALU.add).then_inc(f["y"], 1)

            ffn_vector(fa)
            meet(dve, 0)

            dve.wait_ge(s_w, 16 * 11)
            dve.wait_ge(sbm["vpad"], 2)
            dve.sem_inc(sbm["by"], 4)
            dve.sem_inc(sbm["v"], TPB)
            dve.sem_inc(sbm["l"], 4)
            dve.sem_inc(sbm["gel"], 4)
            dve.sem_inc(b_out, 16 * 12)
            dve.sem_inc(b_vout, 16 * GB)
            with dve.Fori(0, NBLK) as v:
                dve.wait_ge(b_table, 32 * v + 32)
                dve.wait_ge(sbm["turned"], 2 * v + 2)
                for z in range(2):
                    for r, (dst, table) in enumerate(((by_cos, cos_s), (by_sin, sin_s))):
                        a = 2 * z + r
                        dve.wait_ge(sbm["rot_mm"], 4 * v + a + 5)
                        dve.scalar_tensor_tensor(out=dst[:, z, :], in0=psum[:, 3 + a, :], scalar=br4_s[:, a:a + 1],
                                                 in1=table[:, :], op0=ALU.add, op1=ALU.mult).then_inc(sbm["by"], 1)
                dve.wait_ge(b_vout, 16 * GB * (v + 1))
                for t in range(TPB):
                    bank, c0 = (7, 2)[t // 2], (t % 2) * E
                    dve.wait_ge(sbm["v_mm"], TPB * v + 2 * (t // 2) + 2 + TPB)
                    dve.tensor_tensor(vt[:, t, :, 0:HD], psum[:, bank, c0:c0 + E].rearrange("p (h w) -> p h w", h=H),
                                      bv_s[:, :].rearrange("p (h w) -> p h w", h=H), ALU.add).then_inc(sbm["v"], 1)
                for a in range(4):
                    dve.wait_ge(sbm["m"], 4 * v + a + 1)
                    dve.tensor_tensor(part[:, a, 2, :], rest[:, a, :], part[:, a, 1, :],
                                      ALU.subtract).then_inc(sbm["l"], 1)
            meet(dve, 1)

            dve.sem_inc(c_ob, 1)
            for u in range(2):
                dve.sem_inc(c_obst[u], 16)

            def vector_step(kind, u, s, half):
                for e in STEPS[kind]:
                    if e[0] == "max":
                        _, h, i, a, c, width, slot = e
                        v = NMX * s + slot
                        dve.wait_ge(c_mx, v + 1)
                        dve.reduce_max(pmax[:, i % RING, a, c:c + 1], psum[:, 4 + slot % 2, 0:width],
                                       AX_X).then_inc(c_mxread, 1)
                    elif e[0] == "m_fold":
                        _, h, i, slot = e
                        dve.wait_ge(c_mxread, NMX * s + slot)
                        dve.tensor_reduce(nmax[:, i % RING, :], pmax[:, i % RING, :, 0:i + 1], AX_X, ALU.max,
                                          negate=True).then_inc(c_fold, 1)
                    elif e[0] == "m_turn":
                        _, h, i, slot = e
                        v = NMX * s + slot
                        k = HG * NQB * s + NQB * h + i
                        dve.wait_ge(c_mx, v + 1)
                        if not (isinstance(k, int) and k < RING):
                            dve.wait_ge(c_msplit, 4 * (k - RING) + 4)
                        dve.tensor_copy(mrow[:, i % RING, :], psum[0:TPB, 4 + slot % 2, 0:P]).then_inc(c_mxread, 1)
                    elif e[0] == "o_turn":
                        i = e[1]
                        v = NQB * (s - 1) + i
                        dve.wait_ge(c_oturn, v + 2)
                        turned_o = psum[:, 7, :].rearrange("p (g w) -> p g w", w=VW)
                        dve.reciprocal(inv[:, :, :].rearrange("p a h -> p (a h)"),
                                       turned_o[:, :, HD]).then_inc(c_inv, 1)
                        dve.wait_ge(c_inv, v + 1)
                        dve.wait_ge(c_obst[i % 2], 16 * (2 * (s - 1) + i // 2) + 16)
                        dve.tensor_tensor(ob[:, i % 2, :, :].rearrange("p a (h d) -> p (a h) d", h=HG),
                                          turned_o[:, :, 0:HD],
                                          inv[:, :, :].rearrange("p a h -> p (a h)").unsqueeze(2).to_broadcast(
                                              [P, TPB * HG, HD]), ALU.mult).then_inc(c_ob, 1)

            run_steps(dve, vector_step)
            meet(dve, 2)

            dve.sem_inc(d_x2, TPB)
            for t in range(TPB):
                dve.sem_inc(d_out[t], 16)
            with dve.Fori(0, NBLK) as n:
                for t in range(TPB):
                    v, u = TPB * n + t, t % 2
                    dve.wait_ge(d_proj, v + 3)
                    dve.wait_ge(d_x1b, v + 1)
                    dve.wait_ge(d_out[t], 16 * n + 16)
                    dve.tensor_tensor(yt[:, t, :], psum[:, 6 + u, 0:E], x1b[:, u, :], ALU.add).then_inc(d_x2, 1)
            meet(dve, 3)
            ffn_vector(fe)


_ORDER = ["x", "wcq", "bcq", "wqc", "wkc", "wr4", "br4", "bc2", "wv", "bv", "wo", "bo", "wrt", "br", "wet", "be",
          "cos_t", "sin_t"]


def tables():
    import numpy as np
    half = np.arange(0, P, 2, dtype=np.float32) / np.float32(P)
    inv_freq = (np.float32(1.0) / np.power(np.float32(10000.0), half)).astype(np.float32)
    freqs = np.arange(S, dtype=np.float32)[:, None] * inv_freq[None, :]
    emb = np.concatenate([freqs, freqs], axis=-1)
    sign = np.where(np.arange(P) < P // 2, np.float32(-1), np.float32(1))
    return (np.ascontiguousarray(np.cos(emb).T.astype(np.float32)),
            np.ascontiguousarray((np.sin(emb) * sign[None, :]).T.astype(np.float32)))


def kernel(L0_attn_x, L0_attn_wq, L0_attn_bq, L0_attn_wqc, L0_attn_bqc, L0_attn_wqr, L0_attn_bqr, L0_attn_wkv,
           L0_attn_bkv, L0_attn_wkr, L0_attn_bkr, L0_attn_wkc, L0_attn_bkc, L0_attn_wv, L0_attn_bv, L0_attn_wo,
           L0_attn_bo, L0_ffn_Wr, L0_ffn_br, L0_ffn_We, L0_ffn_be):
    import numpy as np
    import concourse.bacc as bacc
    from concourse.bass_utils import run_bass_kernel_spmd

    def arr(a):
        return np.asarray(a)

    def swap(a):
        a = arr(a)
        return np.concatenate([a[..., P // 2:], a[..., :P // 2]], axis=-1)

    cos_t, sin_t = tables()
    data = {
        "x": arr(L0_attn_x).reshape(TOK, E),
        "wcq": np.concatenate([arr(L0_attn_wq), arr(L0_attn_wkv)], axis=1),
        "bcq": np.concatenate([arr(L0_attn_bq), arr(L0_attn_bkv)])[:, None],
        "wqc": arr(L0_attn_wqc),
        "wkc": arr(L0_attn_wkc),
        "wr4": np.stack([arr(L0_attn_wqr), swap(L0_attn_wqr), arr(L0_attn_wkr), swap(L0_attn_wkr)], axis=1),
        "br4": np.stack([arr(L0_attn_bqr), swap(L0_attn_bqr), arr(L0_attn_bkr), swap(L0_attn_bkr)], axis=1),
        "bc2": np.stack([arr(L0_attn_bqc), arr(L0_attn_bkc)], axis=1),
        "wv": arr(L0_attn_wv),
        "bv": arr(L0_attn_bv)[None, :],
        "wo": arr(L0_attn_wo),
        "bo": arr(L0_attn_bo)[None, :],
        "wrt": arr(L0_ffn_Wr).T,
        "br": arr(L0_ffn_br)[None, :],
        "wet": arr(L0_ffn_We).transpose(2, 0, 1).reshape(E, NE * E),
        "be": arr(L0_ffn_be),
        "cos_t": cos_t,
        "sin_t": sin_t,
    }
    nc = bacc.Bacc("TRN2", target_bir_lowering=False, num_devices=1)
    arrays, args = {}, []
    for name in _ORDER:
        a = np.ascontiguousarray(data[name])
        arrays[f"{name}_dram"] = a
        args.append(nc.dram_tensor(f"{name}_dram", a.shape, mybir.dt.from_np(a.dtype), kind="ExternalInput").ap())
    out = nc.dram_tensor("out_dram", (TOK, E), F32, kind="ExternalOutput").ap()
    build(nc, *args, out)
    r = run_bass_kernel_spmd(nc, [arrays], core_ids=[0])
    return r.results[0]["out_dram"].reshape(B, S, E)
```

```python
from contextlib import ExitStack

import concourse.bass as bass
from concourse import mybir

F32 = mybir.dt.float32
BF16 = mybir.dt.bfloat16
F32R = mybir.dt.float32r
ALU = mybir.AluOpType
ACT = mybir.ActivationFunctionType
AX_X = mybir.AxisListType.X

P = 128
B, S, E = 2, 2048, 256
H, DC, HD = 16, 64, 16
NE = 8
KT = E // P
TOK = B * S
BLK = 512
NBLK = TOK // BLK
TPB = BLK // P
NT = TOK // P
NQB = S // BLK
NKT = S // P
HG = 4
NG = B * H // HG
GB = H // HG
PAIRS = HG // 2
VW = 32
FEAT = HG * HD
ROWS = 6 * HD
ROWS_M = ROWS + 3
EPS = 1e-5
SCALE = HD ** -0.5
MASKED = -1.0e30
CONSTS = 9
NPB = 4
RING = 2 * HG
Q_STACK = (0, 1, 2, 0, 1, 0)
K_STACK = (0, 0, 0, 1, 1, 2)
LOADS = len(Q_STACK) + len(K_STACK)
QUADS = [(i, j) for i in range(NQB) for j in range(TPB * i + TPB)]
NQ = len(QUADS)


def first_column(i, j):
    return P * max(0, j - TPB * i)


def maxima(lag, blocks):
    out, late = [], None
    for i in blocks:
        for h in range(HG):
            tasks = []
            for a in range(TPB):
                for c in range(i + 1):
                    width = BLK if c < i else P * (a + 1)
                    tasks.append((("max", lag, h, i, a, c, width), 62 + width / 0.96))
            out += tasks[:2]
            if late:
                out.append(late)
            out += tasks[2:] + [(("m_fold", lag, h, i), 100.0)]
            late = (("m_turn", lag, h, i), 200.0)
    return out + [late]


def plan_step(with_scores, with_max):
    base = []
    if with_scores:
        for n in range(NQ + 1):
            if n < NQ:
                width = BLK - first_column(*QUADS[n])
                base += [(("scores", n, p), 2 * width / 2.4) for p in range(PAIRS)]
            if n >= 1:
                i, j = QUADS[n - 1]
                base.append((("pv", n - 1), HG * (BLK - first_column(i, j)) * 0.46))
                if j == TPB * i + TPB - 1:
                    base.append((("o_out", i), 0.0))
                if j == 0 and i >= 1:
                    base.append((("o_turn", i - 1), 800.0))
        base.append((("o_turn", NQB - 1), 800.0))
    maxes = []
    if with_scores:
        maxes += maxima(1, range(NQB - 1, NQB))
    if with_max:
        maxes += maxima(0, range(NQB - 1))
    total = sum(c for _, c in base) * (1.0 if with_max else 0.5)
    need = sum(c for _, c in maxes)
    order, at, spent = [], 0.0, 0.0
    for event, cost in base:
        while maxes and spent < need * at / total:
            e, c = maxes.pop(0)
            order.append(e)
            spent += c
        order.append(event)
        at += cost
    return order + [e for e, _ in maxes]


def number(order, slot):
    numbered = []
    for event in order:
        if event[0] in ("max", "m_turn", "o_turn"):
            numbered.append((*event, slot))
            slot += 1
        elif event[0] == "m_fold":
            numbered.append((*event, slot))
        else:
            numbered.append(event)
    return numbered


def slots(order):
    return sum(e[0] in ("max", "m_turn", "o_turn") for e in order)


_PLANS = {"max": plan_step(False, True), "both": plan_step(True, True), "scores": plan_step(True, False)}
SLOTS = slots(_PLANS["both"])
FIRST_SLOT = SLOTS - slots(_PLANS["max"])
SHARED = (4, 5, 7)
assert SLOTS % len(SHARED) == 0
STEPS = {kind: number(order, FIRST_SLOT if kind == "max" else 0) for kind, order in _PLANS.items()}
LAST_O_TURN = next(e[-1] for e in STEPS["both"] if e[:2] == ("o_turn", NQB - 1))


def shared_bank(slot):
    return SHARED[slot % len(SHARED)]


def o_turn_before(kind, i):
    return LAST_O_TURN - SLOTS if i == 0 else next(e[-1] for e in STEPS[kind] if e[:2] == ("o_turn", i - 1))


def run_steps(eng, one, between):
    one("max", 0, 0, 0)
    between()
    with eng.Fori(0, (NG - 2) // 2) as k:
        one("both", 1, 2 * k + 1, k)
        one("both", 0, 2 * k + 2, k + 1)
    one("both", 1, NG - 1, NG // 2 - 1)
    one("scores", 0, NG, NG // 2)


def build(nc, x, wcq, bcq, wqc, wkc, wr4, br4, bc2, wv, bv, wo, bo, wrt, br, wet, be, cos_t, sin_t, out):
    with ExitStack() as ctx:
        def sb(name, shape, dt):
            return ctx.enter_context(nc.sbuf_tensor(name, shape, dt))

        def sem(name):
            return ctx.enter_context(nc.semaphore(name))

        def dram(name, shape, dt):
            return nc.dram_tensor(name, shape, dt, kind="Internal").ap()

        psum = ctx.enter_context(nc.psum_tensor("psum", [P, 8, BLK], F32))

        x1_d = dram("x1_d", [TOK, E], F32)
        x2_d = dram("x2_d", [TOK, E], F32)
        q_d = dram("q_d", [3, B * E, S], BF16)
        k_d = dram("k_d", [3, B * E, S], BF16)
        v_d = dram("v_d", [NG, P, NKT, HG * VW], F32)
        att_d = dram("att_d", [NG, S, FEAT], F32)

        ident = sb("ident", [P, P], F32)
        ident_b = sb("ident_b", [P, P], BF16)
        mask_q = sb("mask_q", [P, P], BF16)
        mask_k = sb("mask_k", [P, P], BF16)
        neg_half = sb("neg_half", [P, TPB], F32)
        over_e = sb("over_e", [P, TPB], F32)
        minus_over_e = sb("minus_over_e", [P, TPB], F32)
        eps_s = sb("eps_s", [P, TPB], F32)
        nought = sb("nought", [TPB, P], F32)

        wet_r = sb("wet_r", [P, 2, KT, NE * E], F32R)
        wrt_s = sb("wrt_s", [P, KT, NE], F32)
        wrt_r = sb("wrt_r", [P, KT, 2, NE], F32R)
        br_s = sb("br_s", [P, NE], F32)
        be_s = sb("be_s", [NE, E], F32)
        wcq_s = sb("wcq_s", [P, KT, P], F32)
        wr4_s = sb("wr4_s", [P, KT, 4, P], F32)
        wc2_s = sb("wc2_s", [P, P], F32)
        wv_s = sb("wv_s", [P, E], F32)
        bcq_s = sb("bcq_s", [P, 1], F32)
        bc_s = sb("bc_s", [P, 2], F32)
        br4_s = sb("br4_s", [P, 4], F32)
        bv_s = sb("bv_s", [P, E], F32)
        wo_s = sb("wo_s", [P, KT, E], F32)
        bo_s = sb("bo_s", [P, E], F32)

        xt = sb("xt", [P, TPB, E], F32)
        xc = sb("xc", [P, TPB, E], F32)
        xn = sb("xn", [P, TPB, E], F32)
        unread = sb("unread", [P, TPB, E], F32)
        total = sb("total", [P, TPB], F32)
        neg_mean = sb("neg_mean", [P, TPB], F32)
        squares = sb("squares", [P, TPB], F32)
        mean_sq = sb("mean_sq", [P, TPB], F32)
        variance = sb("variance", [P, TPB], F32)
        rstd = sb("rstd", [P, TPB], F32)
        xnT = sb("xnT", [P, 2, 2, KT, P], F32R)
        gate = sb("gate", [P, 2, NE], F32)
        gate_part = sb("gate_part", [P, 2, NE], F32)
        neg_top = sb("neg_top", [P, 2], F32)
        esum = sb("esum", [P, 2], F32)
        rsum_e = sb("rsum_e", [P, 2], F32)
        expo = sb("expo", [P, 2, NE], F32)
        chosen = sb("chosen", [P, 2, NE], F32)
        half_mask = sb("half_mask", [P, 2, NE], F32)
        maskT = sb("maskT", [NE, 2, P], F32)
        yt = sb("yt", [P, TPB, E], F32)

        with ExitStack() as bctx:
            def sbb(name, shape, dt):
                return bctx.enter_context(nc.sbuf_tensor(name, shape, dt))
            cos_s = sbb("cos_s", [P, BLK], F32)
            sin_s = sbb("sin_s", [P, BLK], F32)
            xnT4 = sbb("xnT4", [P, KT, BLK], F32)
            ccT = sbb("ccT", [P, BLK], F32)
            by_cos = sbb("by_cos", [P, 2, BLK], F32)
            by_sin = sbb("by_sin", [P, 2, BLK], F32)
            turned = sbb("turned", [P, 2, BLK], F32)
            gel = sbb("gel", [P, 4, BLK], F32)
            rest = sbb("rest", [P, 4, BLK], F32)
            part = sbb("part", [P, 4, 3, BLK], BF16)
            vt = sbb("vt", [P, TPB, H, VW], F32)
            wet_s = sbb("wet_s", [P, KT, NE * E], F32)
            att = sbb("att", [P, TPB, GB, FEAT], F32)
            attT = sbb("attT", [P, 2, KT, P], F32)
            x1b = sbb("x1b", [P, 2, E], F32)

        prob = sb("prob", [P, NPB, HG, BLK], F32)
        osb = sb("osb", [P, BLK], F32)
        ob = sb("ob", [P, 2, TPB, FEAT], F32)
        qs_1 = sb("qs_1", [P, HG, S], BF16)
        ks_1 = sb("ks_1", [P, HG, S], BF16)
        vg_1 = sb("vg_1", [P, NKT, HG * VW], F32)
        qs = (sb("qs_0", [P, HG, S], BF16), qs_1)
        ks = (sb("ks_0", [P, HG, S], BF16), ks_1)
        vg = (sb("vg_0", [P, NKT, HG * VW], F32), vg_1)
        pmax = sb("pmax", [P, RING, TPB, NQB], F32)
        nmax = sb("nmax", [P, RING, TPB], F32)
        mrow = sb("mrow", [TPB, RING, P], F32)
        mrest = sb("mrest", [TPB, RING, P], F32)
        mpart = sb("mpart", [TPB, RING, 3, P], BF16)
        inv = sb("inv", [P, TPB, HG], F32)

        s_const0 = sem("s_const0")
        s_const = sem("s_const")
        s_meet = [sem(f"s_meet{n}") for n in range(4)]
        s_router = sem("s_router")
        s_wet = [sem(f"s_wet{c}") for c in range(NE // 2)]
        s_bias = sem("s_bias")
        s_high = sem("s_high")
        s_low = sem("s_low")
        s_w = sem("s_w")

        def ffn_semaphores(tag):
            names = ("total", "negmean", "squares", "variance", "rstd", "xc", "xn", "xn_turned", "high", "low",
                     "logit", "gate", "negtop", "exp", "rsum", "chosen", "mask", "mask_turned", "maskT", "experts",
                     "bias", "y")
            f = {k: sem(f"{tag}_{k}") for k in names}
            f["x_in"] = [sem(f"{tag}_x_in{t}") for t in range(TPB)]
            f["y_out"] = [sem(f"{tag}_y_out{t}") for t in range(TPB)]
            return f

        fa = ffn_semaphores("fa")
        fe = ffn_semaphores("fe")
        b_names = ("total", "negmean", "squares", "variance", "rstd", "xc", "xn", "xn_turned", "xnT", "cc_mm",
                   "cc", "rot_mm", "plain_mm", "v_mm", "by", "turned", "gelp", "gelr", "h", "rest", "m", "l", "v", "vpad")
        sbm = {k: sem(f"b_{k}") for k in b_names}
        b_x = [sem(f"b_x{t}") for t in range(TPB)]
        b_table = sem("b_table")
        b_out = sem("b_out")
        b_vout = sem("b_vout")

        c_stack = [sem(f"c_stack{u}") for u in range(2)]
        c_v = [sem(f"c_v{u}") for u in range(2)]
        c_ones = sem("c_ones")
        c_scores = sem("c_scores")
        c_exp = sem("c_exp")
        c_pv = sem("c_pv")
        c_osb = sem("c_osb")
        c_inv = sem("c_inv")
        c_obst = [sem(f"c_obst{u}") for u in range(2)]
        c_mx = sem("c_mx")
        c_mxread = sem("c_mxread")
        c_fold = sem("c_fold")
        c_msplit = sem("c_msplit")
        c_mst = [[sem(f"c_mst{u}{i}") for i in range(NQB)] for u in range(2)]

        d_att = [sem(f"d_att{t}") for t in range(TPB)]
        d_x1 = [sem(f"d_x1{t}") for t in range(TPB)]
        d_turn = sem("d_turn")
        d_attT = sem("d_attT")
        d_proj = sem("d_proj")
        d_x1b = sem("d_x1b")
        d_x2 = sem("d_x2")
        d_out = [sem(f"d_out{t}") for t in range(TPB)]

        block = ctx.enter_context(nc.Block())

        def meet(eng, n):
            eng.drain().then_inc(s_meet[n], 1)
            eng.wait_ge(s_meet[n], 5)

        def row_number(s, lag, h, i):
            return HG * NQB * (s - lag) + HG * i + h

        def place(h, i):
            return (i % 2) * HG + h

        def uses(half, u):
            return half + u

        @block.sync
        def _(sp):
            def ffn_sync(f, src, dst):
                def blk(n, more):
                    for t in range(TPB):
                        v = TPB * n + t
                        sp.wait_ge(f["y"], 9 * v + 45)
                        sp.dma_start(dst[bass.ts(v, P), :], yt[:, t, :]).then_inc(f["y_out"][t], 16)
                        if more:
                            sp.dma_start(xt[:, t, :], src[bass.ts(v + TPB, P), :]).then_inc(f["x_in"][t], 16)

                with sp.Fori(0, NBLK - 1) as n:
                    blk(n, True)
                blk(NBLK - 1, False)

            def ffn_stored(f):
                for t in range(TPB):
                    sp.wait_ge(f["y_out"][t], 16 * NBLK + 16)

            def ffn_first_loads(f, src, tiles):
                for t in tiles:
                    sp.dma_start(xt[:, t, :], src[t * P:(t + 1) * P, :]).then_inc(f["x_in"][t], 16)

            ffn_first_loads(fa, x, (0, 1))
            sp.dma_start(wrt_s[:, :, :], wrt.rearrange("(k p) n -> p k n", p=P)).then_inc(s_router, 16)
            for c in range(NE // 2):
                sp.dma_start(wet_s[:, :, bass.ts(c, BLK)], wet[:, bass.ts(c, BLK)].rearrange("(k p) n -> p k n", p=P)
                             ).then_inc(s_wet[c], 16)
                if c == 0:
                    sp.dma_start(br_s[:, :], br.to_broadcast([P, NE])).then_inc(s_bias, 16)
                    sp.dma_start(be_s[:, :], be).then_inc(s_bias, 16)
                    ffn_first_loads(fa, x, (2, 3))
            for dst, src in ((wcq_s[:, :, :], wcq.rearrange("(k p) n -> p k n", p=P)),
                             (wr4_s[:, :, :, :], wr4.rearrange("(k p) a n -> p k a n", p=P)),
                             (wc2_s[0:DC, :], wqc), (wc2_s[DC:P, :], wkc), (wv_s[DC:P, :], wv),
                             (bcq_s[:, :], bcq), (bc_s[:, :], bc2), (br4_s[:, :], br4),
                             (bv_s[:, :], bv.to_broadcast([P, E])),
                             (wo_s[:, :, :], wo.rearrange("(k p) n -> p k n", p=P)),
                             (bo_s[:, :], bo.to_broadcast([P, E]))):
                sp.dma_start(dst, src).then_inc(s_w, 16)
            ffn_sync(fa, x, x1_d)

            def load_x1(row):
                for t in range(TPB):
                    sp.dma_start(xt[:, t, :], x1_d[bass.ds(row + t * P, P), :]).then_inc(b_x[t], 16)

            load_x1(0)
            ffn_stored(fa)
            meet(sp, 0)

            def v_is_last(b, n):
                return b == B - 1 and isinstance(n, int) and n == NQB - 1

            def b_sync(b, n, at_b, at_n):
                v = NQB * b + n
                dynamic = not isinstance(n, int)
                row = sp.snap(n * BLK) if dynamic else n * BLK
                nxt = sp.snap((v + 1) * BLK) if dynamic else (v + 1) * BLK
                sp.wait_ge(sbm["by"], 4 * v + 4)
                sp.dma_start(cos_s[:, :], cos_t[:, bass.ds(row, BLK)]).then_inc(b_table, 16)
                sp.dma_start(sin_s[:, :], sin_t[:, bass.ds(row, BLK)]).then_inc(b_table, 16)
                if not v_is_last(b, n):
                    sp.wait_ge(sbm["xn"], TPB * v + TPB)
                    load_x1(nxt)
                if at_b >= 0:
                    store_parts(at_b, at_n, v - 1)
                if v_is_last(b, n):
                    load_group(0, 0)
                sp.wait_ge(sbm["v"], TPB * v + 2 * TPB)
                for g in range(GB):
                    sp.dma_start(v_d[bass.ds(b * GB + g, 1), :, bass.ts(n, TPB), :].rearrange("o p t f -> p (o t) f"),
                                 vt[:, :, g * HG:(g + 1) * HG, :].rearrange("p t h w -> p t (h w)")
                                 ).then_inc(b_vout, 16)

            def store_parts(b, n, v):
                col = n * BLK if isinstance(n, int) else sp.snap(n * BLK)
                sp.wait_ge(sbm["l"], 4 * v + 8)
                for a in range(4):
                    dst = (q_d, k_d)[a % 2]
                    for r in range(3):
                        sp.dma_start(dst[r, bass.ds(b * E + (a // 2) * P, P), bass.ds(col, BLK)],
                                     part[:, a, r, :]).then_inc(b_out, 16)

            def load_group(u, g):
                for dst, src, stack in ((qs[u], q_d, Q_STACK), (ks[u], k_d, K_STACK)):
                    for row, r in enumerate(stack):
                        sp.dma_start(dst[row * HD:(row + 1) * HD, :, :],
                                     src[r, bass.ds(g * FEAT, FEAT), :].rearrange("(h d) s -> d h s", d=HD)
                                     ).then_inc(c_stack[u], 16)
                sp.dma_start(vg[u][:, :, :], v_d[bass.ds(g, 1), :, :, :].rearrange("o p j f -> p (o j) f")
                             ).then_inc(c_v[u], 16)

            for b in range(B):
                b_sync(b, 0, b - 1, NQB - 1)
                with sp.Fori(1, NQB - 1) as n:
                    b_sync(b, n, b, n - 1)
                b_sync(b, NQB - 1, b, NQB - 2)
            store_parts(B - 1, NQB - 1, NBLK - 1)

            def sync_step(kind, u, s, half):
                for e in STEPS[kind]:
                    if e[0] == "m_turn":
                        _, lag, h, i, _ = e
                        k = row_number(s, lag, h, i)
                        z = 1 - u if lag else u
                        sp.wait_ge(c_msplit, 4 * k + 4 + 4 * RING)
                        for r in range(3):
                            sp.dma_start(qs[z][ROWS + r:ROWS + r + 1, h, i * BLK:(i + 1) * BLK],
                                         mpart[:, place(h, i), r, :]).then_inc(c_mst[z][i], 16)
                    elif e[0] == "o_turn":
                        i = e[1]
                        sp.wait_ge(c_mxread, SLOTS * s + e[-1] + 1)
                        sp.dma_start(att_d[bass.ds(s - 1, 1), i * BLK:(i + 1) * BLK, :].rearrange(
                                         "o (a p) f -> p (o a) f", p=P),
                                     ob[:, i % 2, :, :]).then_inc(c_obst[i % 2], 16)
                if kind == "both" and not (isinstance(s, int) and s == NG - 1):
                    sp.wait_ge(c_pv, NQ * s + NPB)
                    load_group(1 - u, s + 1)

            def second_group():
                sp.wait_ge(b_out, 16 * 12 * (NBLK + 1))
                sp.wait_ge(b_vout, 16 * GB * (NBLK + 1))
                meet(sp, 1)
                load_group(1, 1)

            run_steps(sp, sync_step, second_group)
            for u in range(2):
                sp.wait_ge(c_obst[u], 16 * NG * NQB // 2 + 16)
            meet(sp, 2)

            def load_tile(b, n, t):
                row = b * S + n * BLK + t * P
                sp.dma_start(att[:, t, :, :], att_d[b * GB:(b + 1) * GB, bass.ds(n * BLK + t * P, P), :]
                             .rearrange("g p f -> p g f")).then_inc(d_att[t], 16)
                sp.dma_start(xt[:, t, :], x1_d[bass.ds(row, P), :]).then_inc(d_x1[t], 16)

            def d_sync(b, n, next_b, next_n):
                for t in range(TPB):
                    v = (NQB * b + n) * TPB + t
                    sp.wait_ge(d_x2, v + 1 + TPB)
                    if next_b < B:
                        load_tile(next_b, next_n, t)
                    sp.dma_start(x2_d[bass.ts(v, P), :], yt[:, t, :]).then_inc(d_out[t], 16)

            for t in range(TPB):
                load_tile(0, 0, t)
            for b in range(B):
                with sp.Fori(0, NQB - 1) as n:
                    d_sync(b, n, b, n + 1)
                d_sync(b, NQB - 1, b + 1, 0)
            ffn_first_loads(fe, x2_d, range(TPB))
            for t in range(TPB):
                sp.wait_ge(d_out[t], 16 * NBLK + 16)
            meet(sp, 3)
            ffn_sync(fe, x2_d, out)
            ffn_stored(fe)

        @block.gpsimd
        def _(pool):
            pool.memset(ident[:, :], 0.0).then_inc(s_const0, 1)
            pool.memset(mask_q[:, :], 0.0).then_inc(s_const0, 1)
            pool.memset(mask_k[:, :], 0.0).then_inc(s_const0, 1)
            pool.memset(neg_half[:, :], -0.5).then_inc(s_const, 1)
            pool.memset(over_e[:, :], 1.0 / E).then_inc(s_const, 1)
            pool.memset(minus_over_e[:, :], -1.0 / E).then_inc(s_const, 1)
            pool.memset(eps_s[:, :], EPS).then_inc(s_const, 1)
            pool.memset(nought[:, :], 0.0).then_inc(s_const, 1)
            pool.wait_ge(s_const0, 3)
            pool.affine_select(out=ident[:, :], in_=ident[:, :], compare_op=ALU.not_equal, fill=1.0, base=0,
                               pattern=[[-1, P]], channel_multiplier=1).then_inc(s_const, 1)
            pool.affine_select(out=mask_q[:, :], in_=mask_q[:, :], compare_op=ALU.is_ge, fill=MASKED, base=0,
                               pattern=[[-1, P]], channel_multiplier=1).then_inc(s_const, 1)
            pool.affine_select(out=mask_k[:, :], in_=mask_k[:, :], compare_op=ALU.is_ge, fill=MASKED, base=0,
                               pattern=[[1, P]], channel_multiplier=-1).then_inc(s_const, 1)
            pool.wait_ge(s_const, CONSTS - 1)
            pool.tensor_copy(ident_b[:, :], ident[:, :]).then_inc(s_const, 1)

            def statistics(f, t0, t1, v):
                n = t1 - t0
                pool.wait_ge(f["total"], n * v + n)
                pool.tensor_tensor(neg_mean[:, t0:t1], total[:, t0:t1], minus_over_e[:, 0:n],
                                   ALU.mult).then_inc(f["negmean"], 1)
                pool.wait_ge(f["squares"], n * v + n)
                pool.tensor_tensor(mean_sq[:, t0:t1], squares[:, t0:t1], over_e[:, 0:n],
                                   ALU.mult).then_inc(f["variance"], 1)
                pool.wait_ge(f["variance"], 2 * v + 1)
                pool.tensor_tensor(variance[:, t0:t1], mean_sq[:, t0:t1], eps_s[:, 0:n],
                                   ALU.add).then_inc(f["variance"], 1)
                pool.wait_ge(f["variance"], 2 * v + 2)
                pool.tensor_tensor(rstd[:, t0:t1], variance[:, t0:t1], neg_half[:, 0:n],
                                   ALU.pow).then_inc(f["rstd"], 1)

            def ffn_pool(f):
                with pool.Fori(0, NBLK) as n:
                    for t in range(TPB):
                        statistics(f, t, t + 1, TPB * n + t)

            ffn_pool(fa)
            meet(pool, 0)

            def ones(u):
                for h in range(HG):
                    pool.memset(ks[u][ROWS:ROWS_M, h, :], 1.0).then_inc(c_ones, 1)
                pool.wait_ge(c_ones, HG * (u + 1))

            pool.sem_inc(sbm["turned"], 2)
            pool.memset(vt[:, :, :, HD:VW], 0.0).then_inc(sbm["vpad"], 1)
            pool.wait_ge(sbm["vpad"], 1)
            pool.memset(vt[:, :, :, HD:HD + 1], 1.0).then_inc(sbm["vpad"], 1)
            statistics(sbm, 0, TPB, 0)
            pool.wait_ge(sbm["rstd"], 1)
            ones(0)

            def rests(w):
                for a in range(4):
                    pool.wait_ge(sbm["h"], 4 * w + a + 1)
                    pool.wait_ge(sbm["l"], 4 * w + a + 1)
                    pool.tensor_tensor(rest[:, a, :], gel[:, a, :], part[:, a, 0, :],
                                       ALU.subtract).then_inc(sbm["rest"], 1)

            def b_pool(v, before, more):
                if before:
                    rests(v - 1)
                if more:
                    statistics(sbm, 0, TPB, v + 1)
                pool.wait_ge(sbm["gelr"], 2 * v + 2)
                for z in range(2):
                    pool.wait_ge(sbm["by"], 4 * v + 2 * z + 6)
                    pool.tensor_tensor(turned[:, z, :], by_cos[:, z, :], by_sin[:, z, :],
                                       ALU.add).then_inc(sbm["turned"], 1)

            pool.sem_inc(sbm["rest"], 4)
            b_pool(0, False, True)
            with pool.Fori(1, NBLK - 1) as v:
                b_pool(v, True, True)
            b_pool(NBLK - 1, True, False)
            rests(NBLK - 1)

            def second_ones():
                meet(pool, 1)
                ones(1)

            def pool_step(kind, u, s, half):
                for e in STEPS[kind]:
                    if e[0] != "m_turn":
                        continue
                    _, lag, h, i, slot = e
                    k = row_number(s, lag, h, i) + RING
                    r = place(h, i)
                    pool.wait_ge(c_mxread, SLOTS * s + slot + 1)
                    if lag:
                        pool.wait_ge(c_mst[1 - u][i - 2], 48 * HG * uses(half, u))
                    elif i >= 2:
                        pool.wait_ge(c_mst[u][i - 2], 48 * HG * (half + 1))
                    elif kind != "max":
                        pool.wait_ge(c_mst[1 - u][i + 2], 48 * HG * uses(half, u))
                    pool.tensor_tensor(mpart[:, r, 0, :], mrow[:, r, :], nought[:, :],
                                       ALU.subtract).then_inc(c_msplit, 1)
                    pool.wait_ge(c_msplit, 4 * k + 1)
                    pool.tensor_tensor(mrest[:, r, :], mrow[:, r, :], mpart[:, r, 0, :],
                                       ALU.subtract).then_inc(c_msplit, 1)
                    pool.wait_ge(c_msplit, 4 * k + 2)
                    pool.tensor_tensor(mpart[:, r, 1, :], mrest[:, r, :], nought[:, :],
                                       ALU.subtract).then_inc(c_msplit, 1)
                    pool.wait_ge(c_msplit, 4 * k + 3)
                    pool.tensor_tensor(mpart[:, r, 2, :], mrest[:, r, :], mpart[:, r, 1, :],
                                       ALU.subtract).then_inc(c_msplit, 1)

            run_steps(pool, pool_step, second_ones)
            meet(pool, 2)

            with pool.Fori(0, NBLK) as n:
                for t in range(TPB):
                    v = TPB * n + t
                    pool.wait_ge(d_x1[t], 16 * n + 16)
                    pool.wait_ge(d_x2, v + TPB - 1)
                    pool.tensor_tensor(x1b[:, t % 2, :], xt[:, t, :], bo_s[:, :], ALU.add).then_inc(d_x1b, 1)
            meet(pool, 3)
            ffn_pool(fe)

        @block.scalar
        def _(act):
            def normalise(f, x_in, t0, t1, v, n):
                k = t1 - t0
                for t in range(t0, t1):
                    act.wait_ge(x_in[t], 16 * n + 16)
                    act.activation(unread[:, t, :], xt[:, t, :], ACT.Identity,
                                   accum_out=total[:, t:t + 1]).then_inc(f["total"], 1)
                act.wait_ge(f["negmean"], v + 1)
                for t in range(t0, t1):
                    act.activation(xc[:, t, :], xt[:, t, :], ACT.Identity,
                                   bias=neg_mean[:, t:t + 1]).then_inc(f["xc"], 1)
                for t in range(t0, t1):
                    act.wait_ge(f["xc"], k * v + t - t0 + 1)
                    act.activation(unread[:, t, :], xc[:, t, :], ACT.Square,
                                   accum_out=squares[:, t:t + 1]).then_inc(f["squares"], 1)
                act.wait_ge(f["rstd"], v + 1)
                for t in range(t0, t1):
                    act.mul(xn[:, t, :], xc[:, t, :], rstd[:, t:t + 1]).then_inc(f["xn"], 1)

            def ffn_scalar(f):
                def high(v, t):
                    u = t % 2
                    act.wait_ge(f["xn_turned"], v + 1)
                    act.wait_ge(f["experts"], v + 1)
                    act.copy(xnT[:, u, 0, :, :], psum[:, 4 + u, 0:E].rearrange("p (k m) -> p k m", k=KT)
                             ).then_inc(f["high"], 1)

                def blk(n, last):
                    for t in range(TPB):
                        v, u = TPB * n + t, t % 2
                        if t + 2 < TPB:
                            normalise(f, f["x_in"], t + 2, t + 3, v + 2, n)
                        elif not last:
                            normalise(f, f["x_in"], t - 2, t - 1, v + 2, n + 1)
                        act.wait_ge(f["negtop"], v + 1)
                        act.activation(expo[:, u, :], gate[:, u, :], ACT.Exp, bias=neg_top[:, u:u + 1],
                                       accum_out=esum[:, u:u + 1]).then_inc(f["exp"], 1)
                        act.wait_ge(f["mask_turned"], v + 1)
                        act.copy(maskT[:, u, :], psum[0:NE, 6 + u, 384:512]).then_inc(f["maskT"], 1)
                        if not (last and t == TPB - 1):
                            high(v + 1, t + 1)

                normalise(f, f["x_in"], 0, 1, 0, 0)
                if f is fa:
                    split_router()
                    split_high(0)
                normalise(f, f["x_in"], 1, 2, 1, 0)
                high(0, 0)
                if f is fa:
                    for c in range(1, NE // 2):
                        split_high(c)
                with act.Fori(0, NBLK - 1) as n:
                    blk(n, False)
                blk(NBLK - 1, True)

            def split_router():
                act.wait_ge(s_router, 16)
                act.copy(wrt_r[:, :, 0, :], wrt_s[:, :, :]).then_inc(s_high, 1)

            def split_high(c):
                act.wait_ge(s_wet[c], 16)
                for k in range(KT):
                    act.copy(wet_r[:, 0, k, bass.ts(c, BLK)], wet_s[:, k, bass.ts(c, BLK)]).then_inc(s_high, 1)

            act.wait_ge(s_const, CONSTS)
            ffn_scalar(fa)
            meet(act, 0)

            act.wait_ge(s_w, 16 * 11)
            act.sem_inc(sbm["gelp"], 2)
            act.sem_inc(sbm["gelr"], 2)

            def b_scalar(v, more):
                act.wait_ge(sbm["cc_mm"], v + 1)
                act.wait_ge(sbm["v_mm"], TPB * v + TPB)
                act.activation(ccT[:, :], psum[:, 2, :], ACT.Gelu, bias=bcq_s[:, :]).then_inc(sbm["cc"], 1)
                if more:
                    normalise(sbm, b_x, 0, TPB, v + 1, v + 1)
                act.wait_ge(sbm["rest"], 4 * v + 4)
                for z in range(2):
                    act.wait_ge(sbm["plain_mm"], 2 * v + z + 1)
                    act.activation(gel[:, z, :], psum[:, z, :], ACT.Gelu, bias=bc_s[:, z:z + 1]
                                   ).then_inc(sbm["gelp"], 1)
                for z in range(2):
                    act.wait_ge(sbm["turned"], 2 * v + z + 3)
                    act.activation(gel[:, 2 + z, :], turned[:, z, :], ACT.Gelu).then_inc(sbm["gelr"], 1)

            normalise(sbm, b_x, 0, TPB, 0, 0)
            with act.Fori(0, NBLK - 1) as v:
                b_scalar(v, True)
            b_scalar(NBLK - 1, False)
            act.sem_inc(c_exp, 2)
            act.sem_inc(c_osb, 1)

            def scalar_step(kind, u, s, half):
                for e in STEPS[kind]:
                    if e[0] == "scores":
                        _, n, p = e
                        v = NQ * (s - 1) + n
                        c0 = first_column(*QUADS[n])
                        act.wait_ge(c_scores, 2 * v + p + 1)
                        act.wait_ge(c_pv, v + 1)
                        act.activation(prob[:, n % NPB, 2 * p:2 * p + 2, c0:BLK], psum[:, 2 * p:2 * p + 2, c0:BLK],
                                       ACT.Exp, scale=SCALE).then_inc(c_exp, 1)
                    elif e[0] == "o_out":
                        i = e[1]
                        act.wait_ge(c_pv, NQ * (s - 1) + QUADS.index((i, TPB * i + TPB - 1)) + 1 + NPB)
                        act.wait_ge(c_mx, SLOTS * s + o_turn_before(kind, i) + 1)
                        act.copy(osb[:, :], psum[:, 6, :]).then_inc(c_osb, 1)

            run_steps(act, scalar_step, lambda: meet(act, 1))
            meet(act, 2)

            act.sem_inc(d_attT, 2)
            with act.Fori(0, NBLK) as n:
                for t in range(TPB):
                    v, u = TPB * n + t, t % 2
                    act.wait_ge(d_turn, v + 1)
                    act.wait_ge(d_proj, v + 1)
                    act.copy(attT[:, u, :, :], psum[:, 4 + u, 0:E].rearrange("p (k m) -> p k m", k=KT)
                             ).then_inc(d_attT, 1)
            meet(act, 3)
            ffn_scalar(fe)

        @block.tensor
        def _(pe):
            def ffn_tensor(f):
                def halves():
                    return ((k, x, w) for k in range(KT) for x, w in ((0, 0), (0, 1), (1, 0)))

                def turn(v, t):
                    u = t % 2
                    pe.wait_ge(f["xn"], v + 1)
                    pe.wait_ge(f["low"], v + 1)
                    for k in range(KT):
                        last = pe.transpose(psum[:, 4 + u, k * P:(k + 1) * P], xn[:, t, k * P:(k + 1) * P],
                                            ident[:, :])
                    last.then_inc(f["xn_turned"], 1)

                def experts(v, u, c):
                    pe.wait_ge(f["y"], 9 * v + 2 * c + 29)
                    pe.wait_ge(s_low, 1 + KT * (c + 1))
                    for n, (k, x, w) in enumerate(halves()):
                        last = pe.matmul(psum[:, c, :], xnT[:, u, x, k, :], wet_r[:, w, k, c * BLK:(c + 1) * BLK],
                                         start=(n == 0), stop=(n == 3 * KT - 1))
                    last.then_inc(f["experts" if c == NE // 2 - 1 else "bias"], 1)

                def blk(n, last_block):
                    for t in range(TPB):
                        v, u = TPB * n + t, t % 2
                        pe.wait_ge(f["low"], v + 3)
                        experts(v, u, 0)
                        pe.wait_ge(f["y"], 9 * v + 27)
                        pe.wait_ge(s_low, 1)
                        for m, (k, x) in enumerate((k, x) for k in range(KT) for x in range(2)):
                            last = pe.matmul(psum[:, 6 + u, E:E + 2 * NE], xnT[:, u, x, k, :],
                                             wrt_r[:, k, :, :].rearrange("p w n -> p (w n)"),
                                             start=(m == 0), stop=(m == 2 * KT - 1))
                        last.then_inc(f["logit"], 1)
                        experts(v, u, 1)
                        experts(v, u, 2)
                        pe.wait_ge(f["mask"], v + 1)
                        pe.transpose(psum[0:NE, 6 + u, 384:512], half_mask[:, u, :], ident[:, :]
                                     ).then_inc(f["mask_turned"], 1)
                        if not (last_block and t == TPB - 1):
                            turn(v + 1, (t + 1) % TPB)
                        experts(v, u, 3)
                        pe.wait_ge(f["maskT"], v + 1)
                        pe.matmul(psum[:, 6 + u, 0:E], maskT[:, u, :], be_s[:, :], start=True, stop=True
                                  ).then_inc(f["bias"], 1)

                pe.sem_inc(f["experts"], 2)
                turn(0, 0)
                with pe.Fori(0, NBLK - 1) as n:
                    blk(n, False)
                blk(NBLK - 1, True)

            pe.wait_ge(s_const, CONSTS)
            pe.wait_ge(s_bias, 32)
            ffn_tensor(fa)
            meet(pe, 0)

            pe.wait_ge(s_w, 16 * 11)
            pe.sem_inc(sbm["rot_mm"], 4)
            pe.sem_inc(sbm["v_mm"], TPB)
            with pe.Fori(0, NBLK) as v:
                pe.wait_ge(sbm["xn"], TPB * v + TPB)
                pe.wait_ge(sbm["gelp"], 2 * v + 2)
                for k in range(KT):
                    for t in range(TPB):
                        last = pe.transpose(psum[:, k, t * P:(t + 1) * P], xn[:, t, k * P:(k + 1) * P], ident[:, :])
                last.then_inc(sbm["xn_turned"], 1)
                pe.wait_ge(sbm["xnT"], v + 1)
                pe.wait_ge(sbm["v"], TPB * v + TPB)
                for k in range(KT):
                    last = pe.matmul(psum[:, 2, :], wcq_s[:, k, :], xnT4[:, k, :], start=(k == 0), stop=(k == KT - 1))
                last.then_inc(sbm["cc_mm"], 1)
                pe.wait_ge(sbm["by"], 4 * v + 4)
                for a in range(4):
                    for k in range(KT):
                        last = pe.matmul(psum[:, 3 + a, :], wr4_s[:, k, a, :], xnT4[:, k, :],
                                         start=(k == 0), stop=(k == KT - 1))
                    last.then_inc(sbm["rot_mm"], 1)
                pe.wait_ge(sbm["cc"], v + 1)
                for z in range(2):
                    pe.matmul(psum[:, z, :], wc2_s[z * DC:(z + 1) * DC, :], ccT[z * DC:(z + 1) * DC, :],
                              start=True, stop=True).then_inc(sbm["plain_mm"], 1)
                for t in range(TPB):
                    bank, c0 = (7, 2)[t // 2], (t % 2) * E
                    pe.matmul(psum[:, bank, c0:c0 + E], ccT[DC:P, t * P:(t + 1) * P], wv_s[DC:P, :],
                              start=True, stop=True).then_inc(sbm["v_mm"], 1)
            pe.wait_ge(sbm["by"], 4 * NBLK + 4)
            pe.wait_ge(sbm["v"], TPB * NBLK + TPB)
            pe.sem_inc(c_pv, NPB)
            pe.sem_inc(c_mx, FIRST_SLOT)

            def tensor_step(kind, u, s, half):
                w = 1 - u
                for e in STEPS[kind]:
                    if e[0] == "max":
                        _, lag, h, i, a, c, width, slot = e
                        z = w if lag else u
                        bank = shared_bank(slot)
                        if lag == 0 and h == 0 and i == 0 and a == 0:
                            pe.wait_ge(c_stack[u], 16 * LOADS * (half + 1))
                        pe.wait_ge(c_mxread, SLOTS * s + slot - 2)
                        q0 = (TPB * i + a) * P
                        last = pe.matmul(psum[:, bank, 0:width], qs[z][0:ROWS, h, q0:q0 + P],
                                         ks[z][0:ROWS, h, c * BLK:c * BLK + width], start=True, stop=(c < i))
                        if c == i:
                            last = pe.matmul(psum[:, bank, width - P:width], ident_b[:, :], mask_q[:, :],
                                             start=False, stop=True)
                        last.then_inc(c_mx, 1)
                    elif e[0] == "m_turn":
                        _, lag, h, i, slot = e
                        pe.wait_ge(c_fold, row_number(s, lag, h, i) + 1)
                        pe.wait_ge(c_mxread, SLOTS * s + slot - 2)
                        pe.transpose(psum[0:TPB, shared_bank(slot), 0:P], nmax[:, place(h, i), :], ident[:, :]
                                     ).then_inc(c_mx, 1)
                    elif e[0] == "scores":
                        _, n, p = e
                        i, j = QUADS[n]
                        c0 = first_column(i, j)
                        if n == 0 and p == 0:
                            pe.wait_ge(c_ones, HG * (w + 1))
                        if j == 0 and p == 0:
                            pe.wait_ge(c_mst[w][i], 48 * HG * uses(half, u))
                        pe.wait_ge(c_exp, 2 * (NQ * (s - 1) + n) + p + 1)
                        for h in (2 * p, 2 * p + 1):
                            last = pe.matmul(psum[:, h, c0:BLK], ks[w][0:ROWS_M, h, j * P:(j + 1) * P],
                                             qs[w][0:ROWS_M, h, i * BLK + c0:(i + 1) * BLK],
                                             start=True, stop=(j < TPB * i))
                            if j >= TPB * i:
                                last = pe.matmul(psum[:, h, c0:c0 + P], ident_b[:, :], mask_k[:, :],
                                                 start=False, stop=True)
                        last.then_inc(c_scores, 1)
                    elif e[0] == "pv":
                        n = e[1]
                        i, j = QUADS[n]
                        c0 = first_column(i, j)
                        if n == 0:
                            pe.wait_ge(c_v[w], 16 * uses(half, u))
                        if j == 0:
                            pe.wait_ge(c_osb, NQB * (s - 1) + i + 1)
                        pe.wait_ge(c_exp, 2 * (NQ * (s - 1) + n) + 4)
                        for h in range(HG):
                            last = pe.matmul(psum[h * VW:(h + 1) * VW, 6, c0:BLK],
                                             vg[w][:, j, h * VW:(h + 1) * VW], prob[:, n % NPB, h, c0:BLK],
                                             start=(j == 0), stop=(j == TPB * i + TPB - 1), skip_group_check=True)
                        last.then_inc(c_pv, 1)
                    elif e[0] == "o_turn":
                        _, i, slot = e
                        pe.wait_ge(c_osb, NQB * (s - 1) + i + 2)
                        pe.wait_ge(c_mxread, SLOTS * s + slot - 2)
                        for a in range(TPB):
                            last = pe.transpose(psum[:, shared_bank(slot), a * P:(a + 1) * P], osb[:, a * P:(a + 1) * P], ident[:, :])
                        last.then_inc(c_mx, 1)

            run_steps(pe, tensor_step, lambda: meet(pe, 1))
            meet(pe, 2)

            pe.sem_inc(d_proj, 2)

            def turn_heads(n, t):
                v, u = TPB * n + t, t % 2
                pe.wait_ge(d_att[t], 16 * n + 16)
                pe.wait_ge(d_attT, v + 1)
                for k in range(KT):
                    last = pe.transpose(psum[:, 4 + u, k * P:(k + 1) * P],
                                        att[:, t, 2 * k:2 * k + 2, :].rearrange("p g f -> p (g f)"), ident[:, :])
                last.then_inc(d_turn, 1)

            def project(n, last_block):
                for t in range(TPB):
                    v, u = TPB * n + t, t % 2
                    if t + 1 < TPB:
                        turn_heads(n, t + 1)
                    elif not last_block:
                        turn_heads(n + 1, 0)
                    pe.wait_ge(d_attT, v + 3)
                    pe.wait_ge(d_x2, v + TPB - 1)
                    for k in range(KT):
                        last = pe.matmul(psum[:, 6 + u, 0:E], attT[:, u, k, :], wo_s[:, k, :],
                                         start=(k == 0), stop=(k == KT - 1))
                    last.then_inc(d_proj, 1)

            turn_heads(0, 0)
            with pe.Fori(0, NBLK - 1) as n:
                project(n, False)
            project(NBLK - 1, True)
            meet(pe, 3)
            ffn_tensor(fe)

        @block.vector
        def _(dve):
            def ffn_vector(f):
                def low(v, t):
                    u = t % 2
                    dve.wait_ge(f["high"], v + 1)
                    dve.tensor_tensor(xnT[:, u, 1, :, :], psum[:, 4 + u, 0:E].rearrange("p (k m) -> p k m", k=KT),
                                      xnT[:, u, 0, :, :].bitcast(F32), ALU.subtract).then_inc(f["low"], 1)

                def blk(n, last_block):
                    for t in range(TPB):
                        v, u = TPB * n + t, t % 2
                        dve.wait_ge(f["logit"], v + 1)
                        dve.tensor_tensor(gate_part[:, u, :], psum[:, 6 + u, E:E + NE], br_s[:, :],
                                          ALU.add).then_inc(f["gate"], 1)
                        dve.wait_ge(f["gate"], 2 * v + 1)
                        dve.tensor_tensor(gate[:, u, :], psum[:, 6 + u, E + NE:E + 2 * NE], gate_part[:, u, :],
                                          ALU.add).then_inc(f["gate"], 1)
                        dve.wait_ge(f["gate"], 2 * v + 2)
                        dve.reduce_max(neg_top[:, u:u + 1], gate[:, u, :], AX_X, negate=True
                                       ).then_inc(f["negtop"], 1)
                        dve.wait_ge(f["exp"], v + 1)
                        dve.reciprocal(rsum_e[:, u:u + 1], esum[:, u:u + 1]).then_inc(f["rsum"], 1)
                        dve.wait_ge(f["rsum"], v + 1)
                        dve.tensor_scalar(chosen[:, u, :], expo[:, u, :], rsum_e[:, u:u + 1], 0.5, ALU.mult,
                                          ALU.is_gt).then_inc(f["chosen"], 1)
                        dve.wait_ge(f["chosen"], v + 1)
                        dve.tensor_scalar(half_mask[:, u, :], chosen[:, u, :], 0.5, None,
                                          ALU.mult).then_inc(f["mask"], 1)
                        dve.wait_ge(f["mask"], v + 1)
                        dve.wait_ge(f["y_out"][t], 16 * n + 16)
                        for e in range(NE):
                            c = e // 2
                            if e == NE // 2 + 1 and not (last_block and t == TPB - 1):
                                low(v + 1, t + 1)
                            if e == NE - 2:
                                dve.wait_ge(f["experts"], v + 3)
                            elif e % 2 == 0:
                                dve.wait_ge(f["bias"], 4 * v + c + 1)
                            if e:
                                dve.wait_ge(f["y"], 9 * v + e + 36)
                            dve.scalar_tensor_tensor(
                                out=yt[:, t, :], in0=psum[:, c, (e % 2) * E:(e % 2 + 1) * E],
                                scalar=half_mask[:, u, e:e + 1], in1=(yt if e else xt)[:, t, :],
                                op0=ALU.mult, op1=ALU.add).then_inc(f["y"], 1)
                        dve.wait_ge(f["bias"], 4 * v + 4)
                        dve.wait_ge(f["y"], 9 * v + 8 + 36)
                        dve.tensor_tensor(yt[:, t, :], psum[:, 6 + u, 0:E], yt[:, t, :], ALU.add).then_inc(f["y"], 1)

                dve.sem_inc(f["y"], 36)
                dve.sem_inc(f["low"], 2)
                for t in range(TPB):
                    dve.sem_inc(f["y_out"][t], 16)
                low(0, 0)
                if f is fa:
                    for c in range(1, NE // 2):
                        split_low(c)
                with dve.Fori(0, NBLK - 1) as n:
                    blk(n, False)
                blk(NBLK - 1, True)

            def split_low(c):
                for k in range(KT):
                    dve.wait_ge(s_high, 2 + KT * c + k)
                    dve.tensor_tensor(wet_r[:, 1, k, bass.ts(c, BLK)], wet_s[:, k, bass.ts(c, BLK)],
                                      wet_r[:, 0, k, bass.ts(c, BLK)].bitcast(F32), ALU.subtract).then_inc(s_low, 1)

            dve.wait_ge(s_high, 1)
            dve.tensor_tensor(wrt_r[:, :, 1, :], wrt_s[:, :, :], wrt_r[:, :, 0, :].bitcast(F32),
                              ALU.subtract).then_inc(s_low, 1)
            split_low(0)
            dve.wait_ge(s_bias, 32)
            ffn_vector(fa)
            meet(dve, 0)

            dve.wait_ge(s_w, 16 * 11)
            dve.wait_ge(sbm["vpad"], 2)
            dve.sem_inc(sbm["by"], 4)
            dve.sem_inc(sbm["v"], TPB)
            dve.sem_inc(sbm["l"], 4)
            dve.sem_inc(b_out, 16 * 12)
            dve.sem_inc(b_vout, 16 * GB)

            def split(w):
                dve.wait_ge(b_out, 16 * 12 * (w + 1))
                for a in range(4):
                    if a < 2:
                        dve.wait_ge(sbm["gelp"], 2 * w + a + 3)
                    else:
                        dve.wait_ge(sbm["gelr"], 2 * w + a + 1)
                    dve.tensor_copy(part[:, a, 0, :], gel[:, a, :]).then_inc(sbm["h"], 1)
                for a in range(4):
                    dve.wait_ge(sbm["rest"], 4 * w + a + 5)
                    dve.tensor_copy(part[:, a, 1, :], rest[:, a, :]).then_inc(sbm["m"], 1)
                    dve.wait_ge(sbm["m"], 4 * w + a + 1)
                    dve.tensor_tensor(part[:, a, 2, :], rest[:, a, :], part[:, a, 1, :],
                                      ALU.subtract).then_inc(sbm["l"], 1)

            def b_vector(v, before):
                dve.wait_ge(sbm["xn_turned"], v + 1)
                dve.wait_ge(sbm["rot_mm"], 4 * v + 4)
                dve.tensor_copy(xnT4[:, :, :], psum[:, 0:KT, :]).then_inc(sbm["xnT"], 1)
                if before:
                    split(v - 1)
                dve.wait_ge(b_table, 32 * v + 32)
                dve.wait_ge(sbm["turned"], 2 * v + 2)
                for z in range(2):
                    for r, (dst, table) in enumerate(((by_cos, cos_s), (by_sin, sin_s))):
                        a = 2 * z + r
                        dve.wait_ge(sbm["rot_mm"], 4 * v + a + 5)
                        dve.scalar_tensor_tensor(out=dst[:, z, :], in0=psum[:, 3 + a, :], scalar=br4_s[:, a:a + 1],
                                                 in1=table[:, :], op0=ALU.add, op1=ALU.mult).then_inc(sbm["by"], 1)
                dve.wait_ge(b_vout, 16 * GB * (v + 1))
                for t in range(TPB):
                    bank, c0 = (7, 2)[t // 2], (t % 2) * E
                    dve.wait_ge(sbm["v_mm"], TPB * v + 2 * (t // 2) + 2 + TPB)
                    dve.tensor_tensor(vt[:, t, :, 0:HD], psum[:, bank, c0:c0 + E].rearrange("p (h w) -> p h w", h=H),
                                      bv_s[:, :].rearrange("p (h w) -> p h w", h=H), ALU.add).then_inc(sbm["v"], 1)

            b_vector(0, False)
            with dve.Fori(1, NBLK) as v:
                b_vector(v, True)
            split(NBLK - 1)
            dve.sem_inc(c_mxread, FIRST_SLOT)
            dve.sem_inc(c_msplit, 4 * RING)
            for u in range(2):
                dve.sem_inc(c_obst[u], 16)

            def vector_step(kind, u, s, half):
                for e in STEPS[kind]:
                    if e[0] == "max":
                        _, lag, h, i, a, c, width, slot = e
                        dve.wait_ge(c_mx, SLOTS * s + slot + 1)
                        dve.reduce_max(pmax[:, place(h, i), a, c:c + 1], psum[:, shared_bank(slot), 0:width],
                                       AX_X).then_inc(c_mxread, 1)
                    elif e[0] == "m_fold":
                        _, lag, h, i, slot = e
                        r = place(h, i)
                        dve.wait_ge(c_mxread, SLOTS * s + slot)
                        dve.tensor_reduce(nmax[:, r, :], pmax[:, r, :, 0:i + 1], AX_X, ALU.max,
                                          negate=True).then_inc(c_fold, 1)
                    elif e[0] == "m_turn":
                        _, lag, h, i, slot = e
                        dve.wait_ge(c_mx, SLOTS * s + slot + 1)
                        dve.wait_ge(c_msplit, 4 * row_number(s, lag, h, i) + 4)
                        dve.tensor_copy(mrow[:, place(h, i), :], psum[0:TPB, shared_bank(slot), 0:P]).then_inc(c_mxread, 1)
                    elif e[0] == "o_turn":
                        _, i, slot = e
                        v = NQB * (s - 1) + i
                        dve.wait_ge(c_mx, SLOTS * s + slot + 1)
                        dve.wait_ge(c_mxread, SLOTS * s + slot)
                        turned_o = psum[:, shared_bank(slot), :].rearrange("p (g w) -> p g w", w=VW)
                        dve.reciprocal(inv[:, :, :].rearrange("p a h -> p (a h)"),
                                       turned_o[:, :, HD]).then_inc(c_inv, 1)
                        dve.wait_ge(c_inv, v + 1)
                        dve.wait_ge(c_obst[i % 2], 16 * (2 * (s - 1) + i // 2) + 16)
                        dve.tensor_tensor(ob[:, i % 2, :, :].rearrange("p a (h d) -> p (a h) d", h=HG),
                                          turned_o[:, :, 0:HD],
                                          inv[:, :, :].rearrange("p a h -> p (a h)").unsqueeze(2).to_broadcast(
                                              [P, TPB * HG, HD]), ALU.mult).then_inc(c_mxread, 1)

            run_steps(dve, vector_step, lambda: meet(dve, 1))
            meet(dve, 2)

            dve.sem_inc(d_x2, TPB)
            for t in range(TPB):
                dve.sem_inc(d_out[t], 16)
            with dve.Fori(0, NBLK) as n:
                for t in range(TPB):
                    v, u = TPB * n + t, t % 2
                    dve.wait_ge(d_proj, v + 3)
                    dve.wait_ge(d_x1b, v + 1)
                    dve.wait_ge(d_out[t], 16 * n + 16)
                    dve.tensor_tensor(yt[:, t, :], psum[:, 6 + u, 0:E], x1b[:, u, :], ALU.add).then_inc(d_x2, 1)
            meet(dve, 3)
            ffn_vector(fe)


_ORDER = ["x", "wcq", "bcq", "wqc", "wkc", "wr4", "br4", "bc2", "wv", "bv", "wo", "bo", "wrt", "br", "wet", "be",
          "cos_t", "sin_t"]


def tables():
    import numpy as np
    half = np.arange(0, P, 2, dtype=np.float32) / np.float32(P)
    inv_freq = (np.float32(1.0) / np.power(np.float32(10000.0), half)).astype(np.float32)
    freqs = np.arange(S, dtype=np.float32)[:, None] * inv_freq[None, :]
    emb = np.concatenate([freqs, freqs], axis=-1)
    sign = np.where(np.arange(P) < P // 2, np.float32(-1), np.float32(1))
    return (np.ascontiguousarray(np.cos(emb).T.astype(np.float32)),
            np.ascontiguousarray((np.sin(emb) * sign[None, :]).T.astype(np.float32)))


def kernel(L0_attn_x, L0_attn_wq, L0_attn_bq, L0_attn_wqc, L0_attn_bqc, L0_attn_wqr, L0_attn_bqr, L0_attn_wkv,
           L0_attn_bkv, L0_attn_wkr, L0_attn_bkr, L0_attn_wkc, L0_attn_bkc, L0_attn_wv, L0_attn_bv, L0_attn_wo,
           L0_attn_bo, L0_ffn_Wr, L0_ffn_br, L0_ffn_We, L0_ffn_be):
    import numpy as np
    import concourse.bacc as bacc
    from concourse.bass_utils import run_bass_kernel_spmd

    def arr(a):
        return np.asarray(a)

    def swap(a):
        a = arr(a)
        return np.concatenate([a[..., P // 2:], a[..., :P // 2]], axis=-1)

    cos_t, sin_t = tables()
    data = {
        "x": arr(L0_attn_x).reshape(TOK, E),
        "wcq": np.concatenate([arr(L0_attn_wq), arr(L0_attn_wkv)], axis=1),
        "bcq": np.concatenate([arr(L0_attn_bq), arr(L0_attn_bkv)])[:, None],
        "wqc": arr(L0_attn_wqc),
        "wkc": arr(L0_attn_wkc),
        "wr4": np.stack([arr(L0_attn_wqr), swap(L0_attn_wqr), arr(L0_attn_wkr), swap(L0_attn_wkr)], axis=1),
        "br4": np.stack([arr(L0_attn_bqr), swap(L0_attn_bqr), arr(L0_attn_bkr), swap(L0_attn_bkr)], axis=1),
        "bc2": np.stack([arr(L0_attn_bqc), arr(L0_attn_bkc)], axis=1),
        "wv": arr(L0_attn_wv),
        "bv": arr(L0_attn_bv)[None, :],
        "wo": arr(L0_attn_wo),
        "bo": arr(L0_attn_bo)[None, :],
        "wrt": arr(L0_ffn_Wr).T,
        "br": arr(L0_ffn_br)[None, :],
        "wet": arr(L0_ffn_We).transpose(2, 0, 1).reshape(E, NE * E),
        "be": arr(L0_ffn_be),
        "cos_t": cos_t,
        "sin_t": sin_t,
    }
    nc = bacc.Bacc("TRN2", target_bir_lowering=False, num_devices=1)
    arrays, args = {}, []
    for name in _ORDER:
        a = np.ascontiguousarray(data[name])
        arrays[f"{name}_dram"] = a
        args.append(nc.dram_tensor(f"{name}_dram", a.shape, mybir.dt.from_np(a.dtype), kind="ExternalInput").ap())
    out = nc.dram_tensor("out_dram", (TOK, E), F32, kind="ExternalOutput").ap()
    build(nc, *args, out)
    r = run_bass_kernel_spmd(nc, [arrays], core_ids=[0])
    return r.results[0]["out_dram"].reshape(B, S, E)
```
